# Optimizing a Trainium2 kernel written in Bass

```python
import numpy as np
import jax
import jax.numpy as jnp

def _softmax(x, axis=-1):
    return jax.nn.softmax(x, axis=axis)

def _gelu(x):
    return jax.nn.gelu(x, approximate=True)

def _silu(x):
    return jax.nn.silu(x)

def _sigmoid(x):
    return jax.nn.sigmoid(x)

def _layernorm(x, axis=-1, eps=1e-05):
    m = jnp.mean(x, axis=axis, keepdims=True)
    v = jnp.var(x, axis=axis, keepdims=True)
    return (x - m) / jnp.sqrt(v + eps)

def _scatter_add(tgt, idx, src, axis=0):
    return tgt.at[idx].add(src)

def _segment_sum(src, seg, n):
    return jax.ops.segment_sum(src, seg, n)
kernel_name = 'mk_seq_postln_d1_jaxref_r8_906896'

def setup_inputs(seed: int=0):
    np.random.seed(seed)
    _w = jnp.asarray

    def _L0_attn_setup():
        import jax, jax.numpy as jnp
        import numpy as np
        import math
        B, S, D, H = (1, 256, 128, 16)
        HD = D // H
        SCALE = 1.0 / math.sqrt(HD)
        ENT = 0.5
        DECAY = 0.1
        SUP = 0.3
        EPS = 1e-05

        def _heads(x):
            b, s, _ = x.shape
            return x.reshape(b, s, H, HD).transpose(0, 2, 1, 3)
        key = jax.random.key(seed)
        ks = jax.random.split(key, 24)

        def w(k, shape, s=0.02):
            return jax.random.normal(k, shape, dtype=jnp.float32) * s
        return {'hidden_states': jax.random.normal(ks[0], (B, S, D), dtype=jnp.float32), 'Wq': w(ks[1], (D, D)), 'bq': jnp.zeros((D,), jnp.float32), 'Wk': w(ks[2], (D, D)), 'bk': jnp.zeros((D,), jnp.float32), 'Wv': w(ks[3], (D, D)), 'bv': jnp.zeros((D,), jnp.float32), 'Wo': w(ks[4], (D, D)), 'bo': jnp.zeros((D,), jnp.float32), 'Weq': w(ks[5], (D, D), 0.002), 'beq': jnp.zeros((D,), jnp.float32), 'Wek': w(ks[6], (D, D), 0.002), 'bek': jnp.zeros((D,), jnp.float32), 'amp_w': w(ks[7], (H, D)), 'amp_b': jnp.zeros((H,), jnp.float32), 'ph_w': w(ks[8], (H, D)), 'ph_b': jnp.zeros((H,), jnp.float32), 'mix_w': w(ks[9], (H, HD, HD)), 'mix_b': jnp.zeros((H, HD), jnp.float32), 'ln_g': jnp.ones((D,), jnp.float32), 'ln_b': jnp.zeros((D,), jnp.float32)}
    _L0_attn_in = _L0_attn_setup()

    def _L0_ffn_setup():
        import jax, jax.numpy as jnp
        import numpy as np
        FEATURES = 128
        D_IN = 128

        def fp8_gemm_optimized(x, input_scale, kernel, kernel_scale):
            s_in = input_scale[0]
            s_k = kernel_scale[0]
            x_q = (x.astype(jnp.float32) / s_in).astype(jnp.float8_e4m3fn)
            k_q = (kernel.astype(jnp.float32) / s_k).astype(jnp.float8_e4m3fn)
            y = jnp.dot(x_q.astype(jnp.float32), k_q.astype(jnp.float32), preferred_element_type=jnp.float32)
            return y * (s_in * s_k)
        key = jax.random.key(seed)
        kx, kk, kb = jax.random.split(key, 3)
        x = jax.random.normal(kx, (4, 1024, D_IN), dtype=jnp.float32)
        limit = np.sqrt(6.0 / (D_IN + FEATURES)).astype(np.float32)
        kernel = jax.random.uniform(kk, (D_IN, FEATURES), dtype=jnp.float32, minval=-limit, maxval=limit).astype(jnp.bfloat16)
        input_scale = jnp.ones((1,), dtype=jnp.float32)
        kernel_scale = jnp.ones((1,), dtype=jnp.float32)
        bias = jnp.zeros((FEATURES,), dtype=jnp.bfloat16)
        return {'x': x, 'kernel': kernel, 'input_scale': input_scale, 'kernel_scale': kernel_scale, 'bias': bias}
    _L0_ffn_in = _L0_ffn_setup()
    _d = {'L0_attn_hidden_states': _L0_attn_in['hidden_states'], 'L0_attn_Wq': _L0_attn_in['Wq'], 'L0_attn_bq': _L0_attn_in['bq'], 'L0_attn_Wk': _L0_attn_in['Wk'], 'L0_attn_bk': _L0_attn_in['bk'], 'L0_attn_Wv': _L0_attn_in['Wv'], 'L0_attn_bv': _L0_attn_in['bv'], 'L0_attn_Wo': _L0_attn_in['Wo'], 'L0_attn_bo': _L0_attn_in['bo'], 'L0_attn_Weq': _L0_attn_in['Weq'], 'L0_attn_beq': _L0_attn_in['beq'], 'L0_attn_Wek': _L0_attn_in['Wek'], 'L0_attn_bek': _L0_attn_in['bek'], 'L0_attn_amp_w': _L0_attn_in['amp_w'], 'L0_attn_amp_b': _L0_attn_in['amp_b'], 'L0_attn_ph_w': _L0_attn_in['ph_w'], 'L0_attn_ph_b': _L0_attn_in['ph_b'], 'L0_attn_mix_w': _L0_attn_in['mix_w'], 'L0_attn_mix_b': _L0_attn_in['mix_b'], 'L0_attn_ln_g': _L0_attn_in['ln_g'], 'L0_attn_ln_b': _L0_attn_in['ln_b'], 'L0_ffn_kernel': _L0_ffn_in['kernel'], 'L0_ffn_input_scale': _L0_ffn_in['input_scale'], 'L0_ffn_kernel_scale': _L0_ffn_in['kernel_scale'], 'L0_ffn_bias': _L0_ffn_in['bias']}
    _x0 = _d['L0_attn_hidden_states']
    _d['L0_attn_hidden_states'] = jax.random.normal(jax.random.fold_in(jax.random.key(seed), 1), (4, 512, 128), dtype=_x0.dtype)
    del _x0
    return _d

def reference(L0_attn_hidden_states, L0_attn_Wq, L0_attn_bq, L0_attn_Wk, L0_attn_bk, L0_attn_Wv, L0_attn_bv, L0_attn_Wo, L0_attn_bo, L0_attn_Weq, L0_attn_beq, L0_attn_Wek, L0_attn_bek, L0_attn_amp_w, L0_attn_amp_b, L0_attn_ph_w, L0_attn_ph_b, L0_attn_mix_w, L0_attn_mix_b, L0_attn_ln_g, L0_attn_ln_b, L0_ffn_kernel, L0_ffn_input_scale, L0_ffn_kernel_scale, L0_ffn_bias):

    def _L0_attn_ref(hidden_states, Wq, bq, Wk, bk, Wv, bv, Wo, bo, Weq, beq, Wek, bek, amp_w, amp_b, ph_w, ph_b, mix_w, mix_b, ln_g, ln_b):
        import jax, jax.numpy as jnp
        import numpy as np
        import math
        B, S, D, H = (1, 256, 128, 16)
        HD = D // H
        SCALE = 1.0 / math.sqrt(HD)
        ENT = 0.5
        DECAY = 0.1
        SUP = 0.3
        EPS = 1e-05

        def _heads(x):
            b, s, _ = x.shape
            return x.reshape(b, s, H, HD).transpose(0, 2, 1, 3)
        hs = hidden_states
        b, s, _ = hs.shape
        q = _heads(hs @ Wq.T + bq)
        k = _heads(hs @ Wk.T + bk)
        v = _heads(hs @ Wv.T + bv)
        scores = jnp.einsum('bhqd,bhkd->bhqk', q, k) * SCALE
        eq = _heads(hs @ Weq.T + beq)
        ek = _heads(hs @ Wek.T + bek)
        pos = jnp.arange(s)
        decay = jnp.exp(-DECAY * jnp.abs(pos[:, None] - pos[None, :]).astype(jnp.float32))
        esc = jnp.einsum('bhqd,bhkd->bhqk', eq, ek) * (1.0 / math.sqrt(HD)) * decay
        attn = jax.nn.softmax(scores + ENT * esc, axis=-1)
        amps = jax.nn.sigmoid(hs @ amp_w.T + amp_b)
        phases = jnp.tanh(hs @ ph_w.T + ph_b) * math.pi
        a = amps.transpose(0, 2, 1)[..., None]
        p = phases.transpose(0, 2, 1)[..., None]
        sup = jnp.einsum('bhsd,hod->bhso', v, mix_w) + mix_b[None, :, None, :]
        mixed = v + SUP * a * jnp.cos(p) * sup + SUP * a * jnp.sin(p) * jnp.roll(sup, 1, axis=-1)
        ctx = jnp.einsum('bhqk,bhkd->bhqd', attn, mixed)
        ctx = ctx.transpose(0, 2, 1, 3).reshape(b, s, D)
        out = ctx @ Wo.T + bo
        res = hs + out
        mu = jnp.mean(res, axis=-1, keepdims=True)
        var = jnp.mean((res - mu) ** 2, axis=-1, keepdims=True)
        return (res - mu) * jax.lax.rsqrt(var + EPS) * ln_g + ln_b

    def _L0_ffn_ref(x, kernel, input_scale, kernel_scale, bias):
        import jax, jax.numpy as jnp
        import numpy as np
        FEATURES = 128
        D_IN = 128

        def fp8_gemm_optimized(x, input_scale, kernel, kernel_scale):
            s_in = input_scale[0]
            s_k = kernel_scale[0]
            x_q = (x.astype(jnp.float32) / s_in).astype(jnp.float8_e4m3fn)
            k_q = (kernel.astype(jnp.float32) / s_k).astype(jnp.float8_e4m3fn)
            y = jnp.dot(x_q.astype(jnp.float32), k_q.astype(jnp.float32), preferred_element_type=jnp.float32)
            return y * (s_in * s_k)
        dtype = jnp.bfloat16
        x = x.astype(dtype)
        orig_shape = x.shape
        x2 = x.reshape(-1, x.shape[-1])
        y = fp8_gemm_optimized(x2, input_scale, kernel, kernel_scale)
        y = y.astype(dtype) + bias
        return y.reshape(orig_shape[:-1] + (FEATURES,))
    x = L0_attn_hidden_states
    x = _layernorm(x + _L0_attn_ref(x, L0_attn_Wq, L0_attn_bq, L0_attn_Wk, L0_attn_bk, L0_attn_Wv, L0_attn_bv, L0_attn_Wo, L0_attn_bo, L0_attn_Weq, L0_attn_beq, L0_attn_Wek, L0_attn_bek, L0_attn_amp_w, L0_attn_amp_b, L0_attn_ph_w, L0_attn_ph_b, L0_attn_mix_w, L0_attn_mix_b, L0_attn_ln_g, L0_attn_ln_b), axis=-1)
    x = _layernorm(x + _L0_ffn_ref(x, L0_ffn_kernel, L0_ffn_input_scale, L0_ffn_kernel_scale, L0_ffn_bias), axis=-1)
    return x

_drawn_inputs = setup_inputs


def setup_inputs(seed=0):
    import zlib

    import numpy as np

    out = dict(_drawn_inputs(seed))
    spreads = {'L0_attn_bq': (0.0, 0.8),
     'L0_attn_bk': (0.0, 2.0),
     'L0_attn_bv': (0.0, 0.417),
     'L0_attn_bo': (0.0, 0.1),
     'L0_attn_beq': (0.0, 2.0),
     'L0_attn_bek': (0.0, 2.0),
     'L0_attn_amp_b': (0.0, 2.0),
     'L0_attn_ph_b': (0.0, 0.8),
     'L0_attn_mix_b': (0.0, 0.8),
     'L0_attn_ln_g': (1.0, 0.2),
     'L0_attn_ln_b': (0.0, 0.1),
     'L0_ffn_bias': (0.0, 0.1)}
    factors = {'L0_attn_Wq': 8.0,
     'L0_attn_Wk': 8.0,
     'L0_attn_Wv': 8.0,
     'L0_attn_Wo': 3.277,
     'L0_attn_Weq': 64.0,
     'L0_attn_Wek': 64.0,
     'L0_attn_amp_w': 21.673,
     'L0_attn_ph_w': 8.0,
     'L0_attn_mix_w': 8.0}
    for name, (base, spread) in spreads.items():
        noise = np.random.default_rng([zlib.crc32(name.encode()), seed]).standard_normal(out[name].shape)
        drawn = base * np.exp(spread * noise) if base else spread * noise
        out[name] = jnp.asarray(drawn.astype(out[name].dtype))
    for name, factor in factors.items():
        out[name] = (out[name] * factor).astype(out[name].dtype)
    return out
```

```python
import concourse.bass as bass
from concourse import mybir
from contextlib import ExitStack
import math

fp32 = mybir.dt.float32
bf16 = mybir.dt.bfloat16
u32 = mybir.dt.uint32
ALU = mybir.AluOpType
ACT = mybir.ActivationFunctionType

B, S, D, H = 4, 512, 128, 16
HD = D // H
P = 128
NT = S // P
GH = 4
NG = H // GH
CH = 8
R = 2 * HD
TERMS = 6
KR = TERMS * R
MP = 3
SUP, DECAY, ENT, EPS = 0.3, 0.1, 0.5, 1e-5
SCALE = 1.0 / math.sqrt(HD)
NEG = -3.0e38
GROUPS = ((0, 3), (3 * R, 2), (5 * R, 1))


def attention_block(nc, hs, hsT, wqk, bqk, fac_q, fac_k, wv, wv_nat, mixbd, bv_col, mixb, wap, bap,
                    bv_row, wo, bo, ln_g, ln_b, kern, s_in, s_k, fbias, ident, diagfix, kmask,
                    scratch, out):
    ctx = ExitStack()
    with ctx:
        def sb(name, shape, dt=fp32):
            return ctx.enter_context(nc.sbuf_tensor(name, shape, dt))

        def pb(name):
            return ctx.enter_context(nc.psum_tensor(name, [P, 512], fp32))

        def sem(name):
            return ctx.enter_context(nc.semaphore(name))

        hsT_sb = sb("hsT_sb", [P, B * S])
        hs_sb = sb("hs_sb", [P, B * NT, D])
        wqk_sb = sb("wqk_sb", [P, 4, P])
        bqk_sb = sb("bqk_sb", [P, 4])
        fac_sb = [sb("facq_sb", [P, 2, S]), sb("fack_sb", [P, 2, S])]
        bvc_sb = sb("bvc_sb", [P, 1])
        wap_sb = sb("wap_sb", [P, 2 * H])
        bap_sb = sb("bap_sb", [P, 2 * H])
        wo_sb = sb("wo_sb", [P, D])
        bo_sb = sb("bo_sb", [P, D])
        g_sb = sb("g_sb", [P, D])
        b_sb = sb("b_sb", [P, D])
        kern_sb = sb("kern_sb", [P, D], bf16)
        kq_sb = sb("kq_sb", [P, D], bf16)
        sc_sb = sb("sc_sb", [P, 2])
        rs_sb = sb("rs_sb", [P, 2])
        ss_sb = sb("ss_sb", [P, 1])
        fb_sb = sb("fb_sb", [P, D], bf16)
        id_sb = sb("id_sb", [P, P])
        idb_sb = sb("idb_sb", [P, P], bf16)
        fix_sb = sb("fix_sb", [P, P])
        km_sb = sb("km_sb", [P, 2])
        neghalf = sb("neghalf", [P, NT])
        halfpi = sb("halfpi", [P, 1])

        proj = sb("proj", [P, S])
        faced = sb("faced", [P, 2, S])
        parts = sb("parts", [P, 3, 2, S], bf16)

        Qst = sb("Qst", [P, NG, 2, GH, S], bf16)
        Kst = sb("Kst", [P, NG, 2, GH, S], bf16)
        Kd = sb("Kd", [P, 2, 2, S], bf16)
        fixed_all = sb("fixed", [P, NT * (S + P)])
        R_all = sb("R_sb", [P, 2, NT * (S + P)])
        Rm = sb("Rm", [P, 2, GH, NT, P])
        mx = sb("mx", [P, 2, GH * NT])
        mneg = sb("mneg", [P, GH * NT])
        mparts = sb("mparts", [P, P], bf16)
        mrows = sb("mrows", [MP * GH * NT, P], bf16)
        PT = sb("PT", [P, 2, GH, S])
        V = sb("V", [P, B * NT, H, HD])
        Vst = sb("Vst", [P, 2, NT, GH, 32])
        CT = sb("CT", [P, NG, S])

        by_tile = lambda x: x[:, 0:NT * S].rearrange("p (t n) -> p t n", t=NT)
        on_diagonal = lambda x: x[:, :].rearrange("p (t n) -> p t n", t=NT)[:, :, 0:P]
        fixed, fixed_diag = by_tile(fixed_all), on_diagonal(fixed_all)
        scored = [by_tile(R_all[:, i, :]) for i in range(2)]
        scored_diag = [on_diagonal(R_all[:, i, :]) for i in range(2)]
        mpart = lambda i: mparts[:, i * GH * NT:(i + 1) * GH * NT]

        early = PT[:, :, :, :].rearrange("p a b c -> p (a b c)")
        at = [0]

        def lent(n):
            at[0] += n
            return early[:, at[0] - n:at[0]]

        wv_sb = lent(2 * D)
        wvn_sb, mix_sb, bvb_sb = lent(D), lent(D), lent(P)
        bvv_sb = lent(2 * D)
        ap_sb = lent(B * NT * 2 * H).rearrange("p (i n) -> p i n", n=2 * H)
        co_sb = lent(4 * B * NT * H).rearrange("p (k n) -> p k n", k=4)
        VS = Rm[:, :, :, :, :].rearrange("p a b c d -> p (a b c d)").rearrange("p (i n) -> p i n", n=2 * D)
        rden = sb("rden", [P, NT, H])
        x1 = sb("x1", [P, NT, D])
        x2 = sb("x2", [P, NT, D])
        st = sb("st", [P, NT, 6])
        mv = sb("mv", [P, NT, 2])
        ve = sb("ve", [P, NT])
        rstd = sb("rstd", [P, NT])
        q1 = sb("q1", [P, NT, D])
        q2 = sb("q2", [P, NT, D])
        cn = q1
        cnT = q2[:, :, :].rearrange("p t n -> p (t n)")
        xb = sb("xb", [P, NT, D], bf16)
        xq = sb("xq", [P, NT, D], bf16)
        xqT = sb("xqT", [P, S], bf16)

        SB = [pb("SB0"), pb("SB1")]
        EB = pb("EB")
        ST = [pb(f"ST{i}") for i in range(4)]
        CB = pb("CB")
        EBh = EB[:, :].bitcast(bf16)
        ST2h = ST[2][:, :].bitcast(bf16)

        in_first = sem("in_first")
        in_rest = sem("in_rest")
        const_set = sem("const_set")
        proj_ready = sem("proj_ready")
        proj_copied = sem("proj_copied")
        faced_ready = sem("faced_ready")
        hi_ready = sem("hi_ready")
        left_ready = sem("left_ready")
        mid_ready = sem("mid_ready")
        parts_ready = sem("parts_ready")
        parts_stored = sem("parts_stored")
        stacks_in = [sem(f"stacks_in{i}") for i in range(NG)]
        kd_ready = sem("kd_ready")
        e_ready = sem("e_ready")
        fixed_ready = sem("fixed_ready")
        s_ready = sem("s_ready")
        r_ready = sem("r_ready")
        rm_ready = sem("rm_ready")
        msplit = sem("msplit")
        mt_ready = sem("mt_ready")
        mt_copied = sem("mt_copied")
        mrows_in = sem("mrows_in")
        st_ready = sem("st_ready")
        exp_ready = sem("exp_ready")
        v_ready = sem("v_ready")
        pv_ready = sem("pv_ready")
        ct_copied = sem("ct_copied")
        vp_ready = sem("vp_ready")
        vp_copied = sem("vp_copied")
        vprep = sem("vprep")
        vact = sem("vact")
        v_mixed = sem("v_mixed")
        c_pe = sem("c_pe")
        c_dve = sem("c_dve")
        c_pool = sem("c_pool")
        c_act = sem("c_act")
        k_dve = sem("k_dve")
        out_done = sem("out_done")
        passed = sem("passed")

        PE_C, DVE_C, POOL_C, ACT_C = 8, 59, 9, 2

        def hold(eng, s, value):
            if isinstance(value, int):
                if value > 0:
                    eng.wait_ge(s, value)
            else:
                eng.wait_ge(s, value)

        def hold_apart(eng, s, value):
            hold(eng, s, value)
            if not isinstance(value, int):
                eng.sem_inc(passed, 1)

        block = ctx.enter_context(nc.Block())
        NFIRST, NREST = 6, 19

        @block.sync
        def _(sp):
            def take(s, dst, src):
                sp.dma_start(dst, src).then_inc(s, 16)

            take(in_first, wqk_sb[:, :, :], wqk)
            take(in_first, hsT_sb[:, :], hsT)
            take(in_first, bqk_sb[:, :], bqk)
            take(in_first, fac_sb[0][:, :, :], fac_q)
            take(in_first, fac_sb[1][:, :, :], fac_k)
            take(in_first, id_sb[:, :], ident)
            take(in_rest, wap_sb[:, :], wap)
            take(in_rest, wvn_sb[:, :], wv_nat)
            take(in_rest, mix_sb[:, :], mixbd)
            take(in_rest, wv_sb[:, 0:D], wv)
            take(in_rest, bvc_sb[:, :], bv_col)
            take(in_rest, bap_sb[:, :], bap.partition_broadcast(P))
            take(in_rest, bvv_sb[:, 0:D], bv_row.partition_broadcast(P))
            take(in_rest, bvv_sb[:, D:2 * D], mixb.partition_broadcast(P))
            take(in_rest, fix_sb[:, :], diagfix)
            take(in_rest, km_sb[:, :], kmask)
            take(in_rest, hs_sb[:, :, :], hs.rearrange("(i p) d -> p i d", p=P))
            take(in_rest, wo_sb[:, :], wo)
            take(in_rest, bo_sb[:, :], bo.partition_broadcast(P))
            take(in_rest, g_sb[:, :], ln_g.partition_broadcast(P))
            take(in_rest, b_sb[:, :], ln_b.partition_broadcast(P))
            take(in_rest, kern_sb[:, :], kern)
            take(in_rest, fb_sb[:, :], fbias.partition_broadcast(P))
            take(in_rest, sc_sb[:, 0:1], s_in.partition_broadcast(P))
            take(in_rest, sc_sb[:, 1:2], s_k.partition_broadcast(P))

            def store_parts(b, k):
                hold_apart(sp, parts_ready, 4 * b + (k + 1))
                dst = scratch[b, k % 2, k // 2].rearrange("p f r h n -> (r h) (p f) n")
                sp.dma_start(dst, parts[:, :, :, :].rearrange("p a f n -> p (a f) n")).then_inc(parts_stored, 16)

            def load_stacks(b, c):
                bb, g = (b, c) if c < NG else (b + 1, c - NG)
                hold_apart(sp, st_ready, 64 * b + 16 * (c - 3))
                hold_apart(sp, parts_stored, 64 * bb + (32 * (g // 2) + 32))
                for side, st_ in ((0, Qst), (1, Kst)):
                    for f in range(2):
                        src = scratch[bb, side, g // 2, :, f, :, 4 * (g % 2):4 * (g % 2) + 4, :]\
                            .rearrange("p r h n -> r p (h n)")
                        for row, n in GROUPS:
                            part = 3 - n
                            if side == 0:
                                from_ = src[:, part:part + 1, :].broadcast_to([R, n, GH * S])
                            else:
                                from_ = src[:, 0:n, :]
                            sp.dma_start(st_[row:row + n * R, g, f, :, :].rearrange("p j n -> p (j n)"), from_)\
                                .then_inc(stacks_in[g], 16)

            for k in range(4):
                store_parts(0, k)
                if k == 1:
                    load_stacks(0, 0)
                    load_stacks(0, 1)
            load_stacks(0, 2)

            def write_out(b):
                hold_apart(sp, c_dve, DVE_C * b + DVE_C)
                sp.dma_start(out[b].rearrange("(t p) d -> p t d", p=P), x1[:, :, :]).then_inc(out_done, 16)

            def body(b, first=False, last=False):
                for c in range(NG):
                    if c == 0 and not first:
                        write_out(b - 1)
                    if not last:
                        store_parts(b + 1, c)
                    if not last or c == 0:
                        load_stacks(b, c + 3)

            body(0, first=True)
            with sp.Fori(1, B - 1) as b:
                body(b)
            body(B - 1, last=True)
            write_out(B - 1)
            sp.wait_ge(out_done, 16 * B)

        @block.tensor
        def _(pe):
            mm = nc.tensor.matmul

            def project(b, k, wait_sem, wait_value):
                hold(pe, wait_sem, wait_value)
                mm(EB[:, :], wqk_sb[:, k, :], hsT_sb[:, bass.ds(b * S, S)] if not isinstance(b, int)
                   else hsT_sb[:, b * S:b * S + S], start=True, stop=True).then_inc(proj_ready, 1)

            def scores(b, c, j, before_sem, before_value):
                g = c % NG
                u = lambda k, x: k * 4 * b + (k * c + x)
                if j == 0:
                    hold(pe, stacks_in[g], (12 * 16) * b + (12 * 16) * (1 + c // NG))
                hold(pe, kd_ready, u(8, 2 * j + 2))
                hold(pe, before_sem, before_value)
                for t in range(NT):
                    tile = slice(t * P, t * P + P)
                    e = mm(EB[:, tile], Qst[0:KR, g, 0, j, tile], Kd[0:KR, j % 2, 1, tile], start=True, stop=True)
                e.then_inc(e_ready, 1)
                for t in range(NT):
                    tile = slice(t * P, t * P + P)
                    hold(pe, r_ready, u(16, 4 * j + t - 1))
                    bank = SB[t % 2]
                    s = mm(bank[:, tile], Qst[0:KR, g, 0, j, tile], Kd[0:KR, j % 2, 0, tile], start=True, stop=True)
                    if t > 0:
                        s = mm(bank[:, 0:t * P], Qst[0:KR, g, 0, j, tile], Kst[0:KR, g, 0, j, 0:t * P],
                               start=True, stop=True)
                    if t < NT - 1:
                        s = mm(bank[:, (t + 1) * P:S], Qst[0:KR, g, 1, j, tile],
                               Kst[0:KR, g, 1, j, (t + 1) * P:S], start=True, stop=True)
                    s.then_inc(s_ready, 1)

            KM = KR + MP

            def scores_t(b, c, t):
                g = c
                if t == 0:
                    hold(pe, mrows_in, 128 * b + 32 * (c + 1))
                    hold(pe, rm_ready, 16 * b + 4 * (c + 1))
                tile = slice(t * P, t * P + P)
                for j in range(GH):
                    hold(pe, exp_ready, 64 * b + (16 * c + 4 * t + j - 3))
                    bank = ST[j]
                    s = mm(bank[:, tile], Rm[:, c % 2, j, t, :], id_sb[:, :], start=True, stop=True, is_transpose=True)
                    if t < NT - 1:
                        s = mm(bank[:, (t + 1) * P:S], Kst[0:KM, g, 0, j, tile], Qst[0:KM, g, 0, j, (t + 1) * P:S],
                               start=True, stop=True)
                    if t > 0:
                        s = mm(bank[:, 0:t * P], Kst[0:KM, g, 1, j, tile], Qst[0:KM, g, 1, j, 0:t * P],
                               start=True, stop=True)
                    s.then_inc(st_ready, 1)

            def contexts(b, c, t):
                if t == 0:
                    hold(pe, v_ready, 4 * b + (c + 1))
                    hold(pe, ct_copied, 4 * b + c)
                hold(pe, exp_ready, 64 * b + (16 * c + 4 * t + 4))
                for j in range(GH):
                    m = mm(CB[32 * j:32 * j + 32, :], Vst[:, c % 2, t, j, :], PT[:, t % 2, j, :],
                           start=(t == 0), stop=(t == NT - 1))
                m.then_inc(pv_ready, 1)

            def maxima_t(b, c):
                hold(pe, msplit, 16 * b + 4 * (c + 1))
                hold(pe, fixed_ready, 16 * b + 4 * (c + 1))
                mm(EBh[:, 0:P], mparts[:, :], idb_sb[:, :],
                   start=True, stop=True, is_transpose=True).then_inc(mt_ready, 1)

            def ending(b):
                n = lambda x: PE_C * b + x
                hold(pe, exp_ready, 64 * b + 64)
                hold(pe, ct_copied, 4 * b + 4)
                for t in range(NT):
                    for g in range(NG):
                        m = mm(ST[t][:, g * P:g * P + P], CT[:, g, t * P:t * P + P], id_sb[:, :],
                               start=True, stop=True, is_transpose=True)
                    m.then_inc(c_pe, 1)
                hold(pe, c_dve, DVE_C * b + 8)
                for t in range(NT):
                    m = mm(CB[:, t * P:t * P + P], cn[:, t, :], id_sb[:, :], start=True, stop=True, is_transpose=True)
                m.then_inc(c_pe, 1)
                hold(pe, c_act, ACT_C * b + 1)
                for t in range(NT):
                    m = mm(ST[0][:, t * P:t * P + P], cnT[:, t * P:t * P + P], wo_sb[:, :], start=True, stop=True)
                m.then_inc(c_pe, 1)
                hold(pe, c_dve, DVE_C * b + 44)
                for t in range(NT):
                    m = mm(ST2h[:, t * P:t * P + P], xq[:, t, :], idb_sb[:, :], start=True, stop=True, is_transpose=True)
                m.then_inc(c_pe, 1)
                hold(pe, c_act, ACT_C * b + 2)
                for t in range(NT):
                    m = mm(ST[3][:, t * P:t * P + P], xqT[:, t * P:t * P + P], kq_sb[:, :], start=True, stop=True)
                m.then_inc(c_pe, 1)
                hold(pe, c_dve, DVE_C * b + 45)

            pe.wait_ge(in_rest, 16 * NREST)
            mm(ST[0][:, 0:D], wvn_sb[:, :], mix_sb[:, :], start=True, stop=True)
            pe.wait_ge(vprep, 1)
            mm(ST[0][:, D:2 * D], bvb_sb[:, :], mix_sb[:, :], start=True, stop=True).then_inc(vp_ready, 1)
            pe.wait_ge(in_first, 16 * NFIRST)
            for k in range(4):
                project(0, k, proj_copied, k)
            for i in range(B * NT):
                m = mm(ST[1][:, i * 2 * H:(i + 1) * 2 * H], hsT_sb[:, i * P:i * P + P], wap_sb[:, :],
                       start=True, stop=True)
            m.then_inc(vp_ready, 1)
            pe.wait_ge(vprep, 3)
            for i in range(B * NT // 2):
                hold(pe, vp_copied, i - 1)
                for h_ in range(2):
                    m = mm(ST[2 + i % 2][:, h_ * 2 * D:(h_ + 1) * 2 * D],
                           hsT_sb[:, (2 * i + h_) * P:(2 * i + h_ + 1) * P], wv_sb[:, :], start=True, stop=True)
                m.then_inc(vp_ready, 1)
            for j in range(GH):
                scores(0, 0, j, *((proj_copied, 4) if j == 0 else (fixed_ready, j)))
            pe.wait_ge(vp_copied, B * NT // 2)

            def body(b, first=False, last=False):
                for c in range(NG):
                    prev = None if first and c == 0 else ((b, c - 1) if c else (b - 1, NG - 1))
                    if prev:
                        contexts(*prev, NT - 1)
                    maxima_t(b, c)
                    if c == 0 and not first:
                        ending(b - 1)
                    more = not (last and c == NG - 1)
                    for t in range(NT):
                        if more:
                            if t == 0:
                                free = (mt_copied, 4 * b + (c + 1))
                            elif t == 2 and not last:
                                free = (proj_copied, 4 * b + (c + 5))
                            else:
                                free = (fixed_ready, 16 * b + (4 * (c + 1) + t))
                            scores(b, c + 1, t, *free)
                        scores_t(b, c, t)
                        if t > 0:
                            contexts(b, c, t - 1)
                        if t == 1 and not last:
                            project(b + 1, c, fixed_ready, 16 * b + (4 * (c + 1) + 2))

            body(0, first=True)
            with pe.Fori(1, B - 1) as b:
                body(b)
            body(B - 1, last=True)
            contexts(B - 1, NG - 1, NT - 1)
            ending(B - 1)

        @block.scalar
        def _(act):
            def copy_proj(b, k):
                hold(act, proj_ready, 4 * b + (k + 1))
                hold(act, faced_ready, 4 * b + k)
                nc.scalar.activation(proj[:, :], EB[:, :], ACT.Identity, bias=bqk_sb[:, k:k + 1])\
                    .then_inc(proj_copied, 1)

            def cast_hi(b, k):
                hold(act, faced_ready, 4 * b + (k + 1))
                hold(act, parts_stored, 64 * b + 16 * k)
                nc.scalar.activation(parts[:, 0, :, :], faced[:, :, :], ACT.Copy).then_inc(hi_ready, 1)

            def cast_mid(b, k):
                hold(act, left_ready, 4 * b + (k + 1))
                nc.scalar.activation(parts[:, 1, :, :], faced[:, :, :], ACT.Copy).then_inc(mid_ready, 1)

            def place_maxima(b, c):
                hold(act, mt_copied, 4 * b + (c + 1))
                for f in range(2):
                    act.dma_start(Qst[KR:KR + MP, c, f, :, :].rearrange("p j n -> p (j n)"), mrows[:, :])\
                        .then_inc(mrows_in, 16)

            def exps(b, c, t):
                hold(act, pv_ready, 16 * b + (4 * c + t - 1))
                for j in range(GH):
                    hold(act, st_ready, 64 * b + (16 * c + 4 * t + j + 1))
                    nc.scalar.activation(PT[:, t % 2, j, :], ST[j][:, :], ACT.Exp).then_inc(exp_ready, 1)

            def copy_contexts(b, c):
                hold(act, pv_ready, 16 * b + 4 * (c + 1))
                if c == 0:
                    hold(act, c_pe, PE_C * b)
                nc.scalar.activation(CT[:, c, :], CB[:, :], ACT.Copy).then_inc(ct_copied, 1)

            def ending(b):
                hold(act, c_pe, PE_C * b + 5)
                nc.scalar.activation(cnT[:, :], CB[:, :], ACT.Copy).then_inc(c_act, 1)
                hold(act, c_pe, PE_C * b + 7)
                nc.scalar.activation(xqT[:, :], ST2h[:, 0:S], ACT.Copy).then_inc(c_act, 1)

            act.wait_ge(in_first, 16 * NFIRST)
            for k in range(4):
                copy_proj(0, k)
                cast_hi(0, k)
                cast_mid(0, k)
            act.wait_ge(vprep, 4)
            co = lambda i: co_sb[:, i, :].rearrange("p (i h) -> p i h", h=H)
            nc.scalar.activation(co(0), ap_sb[:, :, 0:H], ACT.Exp, scale=-1.0).then_inc(vact, 1)
            nc.scalar.activation(co(1), ap_sb[:, :, H:2 * H], ACT.Tanh).then_inc(vact, 1)
            act.wait_ge(vact, 2)
            nc.scalar.activation(co_sb[:, 2, :], co_sb[:, 1, :], ACT.Sin, scale=math.pi).then_inc(vact, 1)
            act.wait_ge(const_set, 2)
            act.wait_ge(vprep, 5)
            nc.scalar.activation(co_sb[:, 3, :], co_sb[:, 3, :], ACT.Sin, scale=-math.pi, bias=halfpi[:, :])\
                .then_inc(vact, 1)

            def body(b, first=False, last=False):
                for c in range(NG):
                    place_maxima(b, c)
                    if not (first and c == 0):
                        copy_contexts(*((b, c - 1) if c else (b - 1, NG - 1)))
                    if c == 0 and not first:
                        ending(b - 1)
                    for t in range(NT):
                        exps(b, c, t)
                        if not last:
                            if t == 1:
                                copy_proj(b + 1, c)
                            if t == 2:
                                cast_hi(b + 1, c)
                            if t == 3:
                                cast_mid(b + 1, c)

            body(0, first=True)
            with act.Fori(1, B - 1) as b:
                body(b)
            body(B - 1, last=True)
            copy_contexts(B - 1, NG - 1)
            ending(B - 1)

        @block.gpsimd
        def _(pool):
            pool.memset(neghalf[:, :], -0.5).then_inc(const_set, 1)
            pool.memset(halfpi[:, :], math.pi / 2).then_inc(const_set, 1)
            pool.memset(Vst[:, :, :, :, :], 0.0).then_inc(const_set, 1)
            pool.wait_ge(const_set, 3)
            pool.memset(Vst[:, :, :, :, HD:HD + 1], 1.0).then_inc(const_set, 1)
            pool.wait_ge(const_set, 4)
            pool.memset(Kst[KR:KR + MP, :, :, :, :], 1.0).then_inc(const_set, 1)
            pool.wait_ge(in_first, 16 * NFIRST)
            pool.wait_ge(const_set, 5)

            def split(b, k, step):
              if step == 0:
                hold(pool, proj_copied, 4 * b + (k + 1))
                hold(pool, parts_ready, 4 * b + k)
                both = proj[:, :].unsqueeze(1).broadcast_to([P, 2, S])
                nc.gpsimd.tensor_tensor(faced[:, :, :], both, fac_sb[k % 2][:, :, :], ALU.mult)\
                    .then_inc(faced_ready, 1)
              if step == 1:
                hold(pool, hi_ready, 4 * b + (k + 1))
                nc.gpsimd.tensor_tensor(faced[:, :, :], faced[:, :, :], parts[:, 0, :, :], ALU.subtract)\
                    .then_inc(left_ready, 1)
              if step == 2:
                hold(pool, mid_ready, 4 * b + (k + 1))
                nc.gpsimd.tensor_tensor(parts[:, 2, :, :], faced[:, :, :], parts[:, 1, :, :], ALU.subtract)\
                    .then_inc(parts_ready, 1)

            def less_maxima(b, c, j):
                g = c % NG
                hold(pool, r_ready, 16 * (4 * b) + (16 * c + 4 * j + 4))
                hold(pool, st_ready, 16 * (4 * b) + 16 * (c - 1))
                m = mx[:, g % 2, NT * j:NT * j + NT].unsqueeze(2).broadcast_to([P, NT, P])
                nc.gpsimd.tensor_tensor(Rm[:, g % 2, j, :, :], scored_diag[j % 2], m, ALU.subtract).then_inc(rm_ready, 1)

            def place_values(b, c):
                hold_apart(pool, pv_ready, 16 * b + 4 * (c - 1))
                if isinstance(b, int):
                    src = V[:, b * NT:b * NT + NT, c * GH:c * GH + GH, :]
                else:
                    src = V[:, bass.ds(b * NT, NT), c * GH:c * GH + GH, :]
                pool.tensor_copy(Vst[:, c % 2, :, :, 0:HD], src).then_inc(v_ready, 1)

            def ending(b):
                def reciprocal_root(before):
                    hold_apart(pool, c_dve, DVE_C * b + before)
                    pool.tensor_scalar(ve[:, :], mv[:, :, 1], EPS, None, ALU.add).then_inc(c_pool, 1)
                    n[0] += 1
                    hold(pool, c_pool, POOL_C * b + n[0])
                    nc.gpsimd.tensor_tensor(rstd[:, :], ve[:, :], neghalf[:, :], ALU.pow).then_inc(c_pool, 1)
                    n[0] += 1

                n = [0]
                reciprocal_root(18)
                for what, op in ((g_sb, ALU.mult), (b_sb, ALU.add)):
                    if what is g_sb:
                        hold(pool, c_dve, DVE_C * b + 22)
                    else:
                        hold(pool, c_pool, POOL_C * b + n[0])
                    nc.gpsimd.tensor_tensor(x1[:, :, :], x1[:, :, :], what[:, :].unsqueeze(1).broadcast_to([P, NT, D]), op)\
                        .then_inc(c_pool, 1)
                    n[0] += 1
                hold_apart(pool, c_pool, POOL_C * b + n[0])
                h_ = hs_sb[:, b * NT:b * NT + NT, :] if isinstance(b, int) else hs_sb[:, bass.ds(b * NT, NT), :]
                nc.gpsimd.tensor_tensor(x1[:, :, :], x1[:, :, :], h_, ALU.add).then_inc(c_pool, 1)
                n[0] += 1
                reciprocal_root(30)
                reciprocal_root(55)
                assert n[0] == POOL_C

            for k in range(4):
                for step in range(3):
                    split(0, k, step)
            pool.wait_ge(v_mixed, 1)
            for j in range(GH):
                less_maxima(0, 0, j)

            def body(b, first=False, last=False):
                for c in range(NG):
                    place_values(b, c)
                    if c == 0 and not first:
                        ending(b - 1)
                    for j in range(GH):
                        if not (last and c == NG - 1):
                            less_maxima(b, c + 1, j)
                        if j >= 1 and not last:
                            split(b + 1, c, j - 1)

            body(0, first=True)
            with pool.Fori(1, B - 1) as b:
                body(b)
            body(B - 1, last=True)
            ending(B - 1)

        @block.vector
        def _(dve):
            v = nc.vector
            bc = lambda x, n=NT: x[:, :].unsqueeze(1).broadcast_to([P, n, D])
            v.memset(fixed_all[:, :], 0.0).then_inc(k_dve, 1)
            v.memset(mparts[:, :], 0.0).then_inc(k_dve, 1)
            dve.wait_ge(in_rest, 16 * NREST)
            dve.wait_ge(in_first, 16 * NFIRST)
            v.tensor_copy(idb_sb[:, :], id_sb[:, :]).then_inc(k_dve, 1)
            v.tensor_copy(bvb_sb[:, :], bvc_sb[:, 0:1].broadcast_to([P, P])).then_inc(vprep, 1)
            dve.wait_ge(vp_ready, 1)
            v.tensor_copy(wv_sb[:, D:2 * D], ST[0][:, 0:D]).then_inc(vprep, 1)
            v.tensor_tensor(bvv_sb[:, D:2 * D], bvv_sb[:, D:2 * D], ST[0][:, D:2 * D], ALU.add).then_inc(vprep, 1)
            dve.wait_ge(vp_ready, 2)
            v.tensor_tensor(ap_sb[:, :, :], ST[1][:, :].rearrange("p (i n) -> p i n", n=2 * H),
                            bap_sb[:, :].unsqueeze(1).broadcast_to([P, B * NT, 2 * H]), ALU.add).then_inc(vprep, 1)
            dve.wait_ge(vprep, 4)
            for i in range(B * NT // 2):
                dve.wait_ge(vp_ready, 3 + i)
                v.tensor_tensor(VS[:, 2 * i:2 * i + 2, :], ST[2 + i % 2][:, :].rearrange("p (i n) -> p i n", i=2),
                                bvv_sb[:, :].unsqueeze(1).broadcast_to([P, 2, 2 * D]), ALU.add).then_inc(vp_copied, 1)
            dve.wait_ge(vact, 3)
            chain = [5]

            def link(ins):
                chain[0] += 1
                ins.then_inc(vprep, 1)
                dve.wait_ge(vprep, chain[0])

            v.tensor_scalar(co_sb[:, 3, :].bitcast(u32), co_sb[:, 1, :].bitcast(u32), 0x7FFFFFFF, None, ALU.bitwise_and).then_inc(vprep, 1)
            dve.wait_ge(vprep, 5)
            link(v.tensor_scalar(co_sb[:, 0, :], co_sb[:, 0, :], 1.0, None, ALU.add))
            link(v.reciprocal(co_sb[:, 0, :], co_sb[:, 0, :]))
            link(v.tensor_scalar(co_sb[:, 0, :], co_sb[:, 0, :], SUP, None, ALU.mult))
            dve.wait_ge(vact, 4)
            dve.wait_ge(vp_copied, B * NT // 2)
            link(v.tensor_tensor(co_sb[:, 3, :], co_sb[:, 3, :], co_sb[:, 0, :], ALU.mult))
            link(v.tensor_tensor(co_sb[:, 2, :], co_sb[:, 2, :], co_sb[:, 0, :], ALU.mult))
            NI = B * NT
            sup = VS[:, :, D:2 * D].rearrange("p i (h d) -> p i h d", d=HD)
            val = VS[:, :, 0:D].rearrange("p i (h d) -> p i h d", d=HD)
            fac = lambda i, n: co_sb[:, i, :].rearrange("p (i h) -> p i h", h=H).unsqueeze(3).broadcast_to([P, NI, H, n])
            link(v.tensor_tensor(V[:, :, :, :], sup, fac(3, HD), ALU.mult))
            link(v.tensor_tensor(val, val, V[:, :, :, :], ALU.add))
            v.tensor_tensor(V[:, :, :, 1:HD], sup[:, :, :, 0:HD - 1], fac(2, HD - 1), ALU.mult).then_inc(vprep, 1)
            chain[0] += 1
            link(v.tensor_tensor(V[:, :, :, 0:1], sup[:, :, :, HD - 1:HD], fac(2, 1), ALU.mult))
            v.tensor_tensor(V[:, :, :, :], val, V[:, :, :, :], ALU.add).then_inc(v_mixed, 1)

            kk = [3]

            def klink(ins):
                kk[0] += 1
                ins.then_inc(k_dve, 1)
                dve.wait_ge(k_dve, kk[0])

            klink(v.reciprocal(rs_sb[:, :], sc_sb[:, :]))
            klink(v.tensor_tensor(ss_sb[:, :], sc_sb[:, 0:1], sc_sb[:, 1:2], ALU.mult))

            def quantize(dst, src, a, t1, t2, scale, step):
                step(v.tensor_scalar(a, src, scale, None, ALU.mult))
                step(v.tensor_scalar(t1.bitcast(u32), a.bitcast(u32), 0x7F800000, None, ALU.bitwise_and))
                step(v.tensor_scalar(t1, t1, 2.0 ** -6, 1.5 * 2.0 ** 20, ALU.max, ALU.mult))
                step(v.tensor_tensor(a, a, t1, ALU.add))
                step(v.tensor_tensor(a, a, t1, ALU.subtract))
                step(v.tensor_tensor(t1, a, a, ALU.mult))
                step(v.tensor_scalar(t1, t1, 448.0 ** 2, 3e38, ALU.is_gt, ALU.mult))
                step(v.tensor_scalar(t1, t1, 3e38, 0.0, ALU.mult, ALU.mult))
                step(v.tensor_tensor(dst, a, t1, ALU.add))

            quantize(kq_sb[:, :], kern_sb[:, :], q1[:, 0, :], q2[:, 0, :], None, rs_sb[:, 1:2], klink)
            NK = kk[0]

            def k_stacks(b, c, j):
                g = c % NG
                if j == 0:
                    hold(dve, stacks_in[g], (12 * 16) * b + (12 * 16) * (1 + c // NG))
                hold(dve, s_ready, 64 * b + (16 * c + 4 * j - 4))
                for s in range(2):
                    v.tensor_scalar(Kd[0:KR, j % 2, s, :], Kst[0:KR, g, 0, j, :], km_sb[0:KR, s:s + 1], None, ALU.mult)\
                        .then_inc(kd_ready, 1)

            def head(b, c, j):
                g = c % NG
                hold(dve, e_ready, 16 * b + (4 * c + j + 1))
                hold(dve, r_ready, 64 * b + (16 * c + 4 * j))
                v.tensor_tensor(fixed_diag, EB[:, :].rearrange("p (t n) -> p t n", t=NT), bc(fix_sb), ALU.mult)\
                    .then_inc(fixed_ready, 1)
                for t in range(NT):
                    hold_apart(dve, s_ready, 64 * b + (16 * c + 4 * j + t + 1))
                    if t == 0:
                        hold_apart(dve, fixed_ready, 16 * b + (4 * c + j + 1))
                        hold_apart(dve, rm_ready, 16 * b + (4 * c + j - 1))
                    v.tensor_tensor_reduce(out=scored[j % 2][:, t, :], in0=SB[t % 2][:, :], in1=fixed[:, t, :], scale=1.0,
                                           scalar=NEG, op0=ALU.add, op1=ALU.max,
                                           accum_out=mx[:, g % 2, NT * j + t:NT * j + t + 1]).then_inc(r_ready, 1)

            def split_maxima(b, c):
                g = c % NG
                m = mx[:, g % 2, :]
                x = lambda k: 16 * b + (4 * c + k)
                hold(dve, r_ready, 64 * b + (16 * c + 16))
                hold(dve, mt_ready, 4 * b + c)
                v.tensor_scalar(mpart(0), m, -1.0, None, ALU.mult).then_inc(msplit, 1)
                hold(dve, msplit, x(1))
                v.scalar_tensor_tensor(out=mneg[:, :], in0=m, scalar=-1.0, in1=mpart(0),
                                       op0=ALU.mult, op1=ALU.subtract).then_inc(msplit, 1)
                hold(dve, msplit, x(2))
                v.tensor_copy(mpart(1), mneg[:, :]).then_inc(msplit, 1)
                hold(dve, msplit, x(3))
                v.tensor_tensor(mpart(2), mneg[:, :], mpart(1), ALU.subtract).then_inc(msplit, 1)

            def copy_maxima(b, c):
                hold(dve, mt_ready, 4 * b + (c + 1))
                hold(dve, mrows_in, 128 * b + 32 * c)
                v.tensor_copy(mrows[:, :], EBh[0:MP * GH * NT, 0:P]).then_inc(mt_copied, 1)

            def ending(b):
                n = [0]

                def step(ins, chained=True):
                    n[0] += 1
                    ins.then_inc(c_dve, 1)
                    if chained:
                        settle()

                def settle():
                    hold_apart(dve, c_dve, DVE_C * b + n[0])

                for t in range(NT):
                    hold(dve, c_pe, PE_C * b + t + 1)
                    parts_ = ST[t][:, :].rearrange("p (h n) -> p h n", n=32)
                    v.reciprocal(rden[:, t, :], parts_[:, :, HD]).then_inc(c_dve, 1)
                    n[0] += 1
                    hold(dve, c_dve, DVE_C * b + n[0])
                    step(v.tensor_tensor(cn[:, t, :].rearrange("p (h d) -> p h d", d=HD), parts_[:, :, 0:HD],
                                         rden[:, t, :].unsqueeze(2).broadcast_to([P, H, HD]), ALU.mult), False)
                assert n[0] == 8
                hold(dve, c_pe, PE_C * b + 6)
                hold(dve, out_done, 16 * b)
                step(v.tensor_tensor(x1[:, :, :], ST[0][:, :].rearrange("p (t n) -> p t n", t=NT), bc(bo_sb), ALU.add))
                h_ = hs_sb[:, b * NT:b * NT + NT, :] if isinstance(b, int) else hs_sb[:, bass.ds(b * NT, NT), :]
                step(v.tensor_tensor(x1[:, :, :], x1[:, :, :], h_, ALU.add))

                def stats(x):
                    for t in range(NT):
                        step(v.bn_stats(st[:, t, :], x[:, t, :]), False)
                    settle()
                    for t in range(NT):
                        step(v.bn_aggr(mv[:, t, :], st[:, t, :]), False)

                def normalize(dst, x, ready):
                    hold(dve, c_dve, DVE_C * b + n[0])
                    hold_apart(dve, c_pool, POOL_C * b + ready)
                    for t in range(NT):
                        step(v.tensor_scalar(dst[:, t, :], x[:, t, :], mv[:, t, 0:1], rstd[:, t:t + 1],
                                             ALU.subtract, ALU.mult), t == NT - 1)

                stats(x1)
                assert n[0] == 18, n[0]
                normalize(x1, x1, 2)
                hold_apart(dve, c_pool, POOL_C * b + 5)
                stats(x1)
                normalize(x2, x1, 7)
                step(v.tensor_copy(xb[:, :, :], x2[:, :, :]))
                quantize(xq[:, :, :], xb[:, :, :], q1[:, :, :], q2[:, :, :], None, rs_sb[:, 0:1], step)
                hold(dve, c_pe, PE_C * b + PE_C)
                step(v.tensor_scalar(xb[:, :, :], ST[3][:, :].rearrange("p (t n) -> p t n", t=NT), ss_sb[:, 0:1], None,
                                     ALU.mult))
                step(v.tensor_tensor(xb[:, :, :], xb[:, :, :], bc(fb_sb), ALU.add))
                step(v.tensor_tensor(x2[:, :, :], x2[:, :, :], xb[:, :, :], ALU.add))
                stats(x2)
                normalize(x1, x2, 9)
                return n[0]

            dve.wait_ge(k_dve, NK)
            for j in range(GH):
                k_stacks(0, 0, j)
                if j:
                    head(0, 0, j - 1)
            head(0, 0, GH - 1)
            split_maxima(0, 0)

            def body(b, first=False, last=False):
                for c in range(NG):
                    copy_maxima(b, c)
                    if c == 0 and not first:
                        ending(b - 1)
                    if not (last and c == NG - 1):
                        for j in range(GH):
                            k_stacks(b, c + 1, j)
                            if j:
                                head(b, c + 1, j - 1)
                        head(b, c + 1, GH - 1)
                        split_maxima(b, c + 1)

            body(0, first=True)
            with dve.Fori(1, B - 1) as b:
                body(b)
            body(B - 1, last=True)
            ending(B - 1)


def _constants(np):
    pos = np.arange(S) - (S - 1) / 2
    far = np.exp(-DECAY * pos)
    fac_q, fac_k = np.ones((2, P, 2, S))
    fac_q[:HD * CH] = SCALE
    fac_q[HD * CH:, 0], fac_q[HD * CH:, 1] = ENT * SCALE * far, ENT * SCALE / far
    fac_k[HD * CH:, 0], fac_k[HD * CH:, 1] = 1 / far, far
    q, k = np.arange(P)[:, None], np.arange(P)[None, :]
    diagfix = np.where(q >= k, 1.0, np.exp(-2 * DECAY * (k - q)))
    kmask = np.zeros((P, 2))
    for row, n in GROUPS:
        for i in range(n * R):
            kmask[row + i, i // n // HD] = 1
    return {"fac_q": fac_q, "fac_k": fac_k, "ident": np.eye(P), "diagfix": diagfix, "kmask": kmask}


def kernel(**inputs):
    import numpy as np
    import concourse.bacc as _bacc
    from concourse.bass_utils import run_bass_kernel_spmd as _run

    a = {n.removeprefix("L0_"): np.asarray(x) for n, x in inputs.items()}
    w = {n.removeprefix("attn_"): x for n, x in a.items()}
    f32 = np.float32
    tokens = w["hidden_states"].reshape(B * S, D)

    def chunked(x, kind):
        return x.reshape(H // CH, CH, HD, *x.shape[1:]).swapaxes(1, 2)

    def rows(plain, entangled):
        x = np.concatenate([chunked(plain, 0), chunked(entangled, 1)], axis=1)
        return x.reshape(H // CH, P, *x.shape[3:])

    wq, wk = rows(w["Wq"], w["Weq"]), rows(w["Wk"], w["Wek"])
    bq, bk = rows(w["bq"], w["beq"]), rows(w["bk"], w["bek"])
    mixbd = np.zeros((H, HD, H, HD), f32)
    for h in range(H):
        mixbd[h, :, h, :] = w["mix_w"][h].T
    arrays = {
        "hs": tokens, "hsT": tokens.T,
        "wqk": np.stack([wq[0], wk[0], wq[1], wk[1]]).transpose(2, 0, 1),
        "bqk": np.stack([bq[0], bk[0], bq[1], bk[1]]).T,
        "wv": w["Wv"].T, "wv_nat": w["Wv"], "mixbd": mixbd.reshape(D, D), "bv_col": w["bv"].reshape(D, 1),
        "mixb": w["mix_b"].reshape(D), "wap": np.concatenate([w["amp_w"], w["ph_w"]]).T,
        "bap": np.concatenate([w["amp_b"], w["ph_b"]]), "bv_row": w["bv"], "wo": w["Wo"].T, "bo": w["bo"],
        "ln_g": w["ln_g"], "ln_b": w["ln_b"], "kern": w["ffn_kernel"], "s_in": w["ffn_input_scale"],
        "s_k": w["ffn_kernel_scale"], "fbias": w["ffn_bias"],
    }
    arrays.update({n: x.astype(f32) for n, x in _constants(np).items()})
    arrays = {f"in_{n}": np.ascontiguousarray(x) for n, x in arrays.items()}

    nc = _bacc.Bacc("TRN2", target_bir_lowering=False, num_devices=1)
    args = {n.removeprefix("in_"): nc.dram_tensor(n, x.shape, mybir.dt.from_np(x.dtype), kind="ExternalInput").ap()
            for n, x in arrays.items()}
    scratch = nc.dram_tensor("stacks", (B, 2, H // CH, 3, 2, R, CH, S), bf16, kind="Internal").ap()
    out = nc.dram_tensor("out", (B, S, D), fp32, kind="ExternalOutput").ap()
    attention_block(nc, scratch=scratch, out=out, **args)
    r = _run(nc, [arrays], core_ids=[0])
    return r.results[0]["out"]
```

```python
import concourse.bass as bass
from concourse import mybir
from contextlib import ExitStack
import math

fp32 = mybir.dt.float32
bf16 = mybir.dt.bfloat16
u32 = mybir.dt.uint32
ALU = mybir.AluOpType
ACT = mybir.ActivationFunctionType

B, S, D, H = 4, 512, 128, 16
HD = D // H
P = 128
NT = S // P
GH = 4
NG = H // GH
CH = 8
R = 2 * HD
TERMS = 6
KR = TERMS * R
MP = 3
SUP, DECAY, ENT, EPS = 0.3, 0.1, 0.5, 1e-5
SCALE = 1.0 / math.sqrt(HD)
NEG = -3.0e38
GROUPS = ((0, 3), (3 * R, 2), (5 * R, 1))


def attention_block(nc, hs, hsT, wqk, bqk, fac_q, fac_k, wv, wv_nat, mixbd, bv_col, mixb, wap, bap,
                    bv_row, wo, bo, ln_g, ln_b, kern, s_in, s_k, fbias, ident, diagfix, kmask,
                    scratch, out):
    ctx = ExitStack()
    with ctx:
        def sb(name, shape, dt=fp32):
            return ctx.enter_context(nc.sbuf_tensor(name, shape, dt))

        def pb(name):
            return ctx.enter_context(nc.psum_tensor(name, [P, 512], fp32))

        def sem(name):
            return ctx.enter_context(nc.semaphore(name))

        hsT_sb = sb("hsT_sb", [P, B * S])
        hs_sb = sb("hs_sb", [P, B * NT, D])
        wqk_sb = sb("wqk_sb", [P, 4, P])
        bqk_sb = sb("bqk_sb", [P, 4])
        fac_sb = [sb("facq_sb", [P, 2, S]), sb("fack_sb", [P, 2, S])]
        bvc_sb = sb("bvc_sb", [P, 1])
        wap_sb = sb("wap_sb", [P, 2 * H])
        bap_sb = sb("bap_sb", [P, 2 * H])
        wo_sb = sb("wo_sb", [P, D])
        bo_sb = sb("bo_sb", [P, D])
        g_sb = sb("g_sb", [P, D])
        b_sb = sb("b_sb", [P, D])
        kern_sb = sb("kern_sb", [P, D], bf16)
        kq_sb = sb("kq_sb", [P, D], bf16)
        sc_sb = sb("sc_sb", [P, 2])
        rs_sb = sb("rs_sb", [P, 2])
        ss_sb = sb("ss_sb", [P, 1])
        fb_sb = sb("fb_sb", [P, D], bf16)
        id_sb = sb("id_sb", [P, P])
        idb_sb = sb("idb_sb", [P, P], bf16)
        fix_sb = sb("fix_sb", [P, P])
        km_sb = sb("km_sb", [P, 2])
        neghalf = sb("neghalf", [P, NT])
        halfpi = sb("halfpi", [P, 1])

        proj = sb("proj", [P, S])
        faced = sb("faced", [P, 2, S])
        parts = sb("parts", [P, 2, 3, S], bf16)

        Qst = sb("Qst", [P, NG, 2, GH, S], bf16)
        Kst = sb("Kst", [P, NG, 2, GH, S], bf16)
        Kd = sb("Kd", [P, 2, 2, S], bf16)
        fixed_all = sb("fixed", [P, NT * (S + P)])
        R_all = sb("R_sb", [P, 2, NT * (S + P)])
        Rm = sb("Rm", [P, 2, GH, NT, P])
        mx = sb("mx", [P, 2, GH * NT])
        mneg = sb("mneg", [P, GH * NT])
        mparts = sb("mparts", [P, P], bf16)
        mrows = sb("mrows", [MP * GH * NT, P], bf16)
        PT = sb("PT", [P, 2, GH, S])
        V = sb("V", [P, B * NT, H, HD])
        Vst = sb("Vst", [P, 2, NT, GH, 32])
        CT = sb("CT", [P, NG, S])

        by_tile = lambda x: x[:, 0:NT * S].rearrange("p (t n) -> p t n", t=NT)
        on_diagonal = lambda x: x[:, :].rearrange("p (t n) -> p t n", t=NT)[:, :, 0:P]
        fixed, fixed_diag = by_tile(fixed_all), on_diagonal(fixed_all)
        scored = [by_tile(R_all[:, i, :]) for i in range(2)]
        scored_diag = [on_diagonal(R_all[:, i, :]) for i in range(2)]
        mpart = lambda i: mparts[:, i * GH * NT:(i + 1) * GH * NT]

        R_flat = R_all[:, :, :].rearrange("p a b -> p (a b)")
        faced_early = R_flat[:, 0:2 * S].rearrange("p (f n) -> p f n", f=2)
        parts_early = [R_flat[:, (2 + 3 * i) * S:(5 + 3 * i) * S].bitcast(bf16).rearrange("p (f a n) -> p f a n", f=2, a=3)
                       for i in range(2)]

        early = PT[:, :, :, :].rearrange("p a b c -> p (a b c)")
        at = [0]

        def lent(n):
            at[0] += n
            return early[:, at[0] - n:at[0]]

        wv_sb = lent(2 * D)
        wvn_sb, mix_sb, bvb_sb = lent(D), lent(D), lent(P)
        bvv_sb = lent(2 * D)
        ap_sb = lent(B * NT * 2 * H).rearrange("p (i n) -> p i n", n=2 * H)
        co_sb = lent(4 * B * NT * H).rearrange("p (k n) -> p k n", k=4)
        VS = [x.rearrange("p (i n) -> p i n", n=2 * D) for x in
              (Qst[:, NG - 1, :, :, :].rearrange("p f j n -> p (f j n)").bitcast(fp32),
               Rm[:, 1, :, :, :].rearrange("p j t n -> p (j t n)"))]
        HALF = B * NT // 2
        rden = sb("rden", [P, NT, H])
        x1 = sb("x1", [P, NT, D])
        x2 = sb("x2", [P, NT, D])
        st = sb("st", [P, NT, 6])
        mv = sb("mv", [P, NT, 2])
        ve = sb("ve", [P, NT])
        rstd = sb("rstd", [P, NT])
        q1 = sb("q1", [P, NT, D])
        q2 = sb("q2", [P, NT, D])
        cn = q1
        cnT = q2[:, :, :].rearrange("p t n -> p (t n)")
        xb = sb("xb", [P, NT, D], bf16)
        xq = sb("xq", [P, NT, D], bf16)
        xqT = sb("xqT", [P, S], bf16)

        SB = [pb(f"SB{i}") for i in range(3)]
        EB = pb("EB")
        ST = [pb("ST0"), pb("ST1")]
        CB = pb("CB")
        MB = pb("MB")
        VP = [CB, SB[2]]
        MBh = MB[:, :].bitcast(bf16)

        in_first = sem("in_first")
        in_rest = sem("in_rest")
        in_late = sem("in_late")
        ones_set = sem("ones_set")
        early_ready = sem("early_ready")
        early_split = sem("early_split")
        early_stored = sem("early_stored")
        const_set = sem("const_set")
        proj_ready = sem("proj_ready")
        proj_copied = sem("proj_copied")
        faced_ready = sem("faced_ready")
        hi_ready = sem("hi_ready")
        left_ready = sem("left_ready")
        mid_ready = sem("mid_ready")
        parts_ready = sem("parts_ready")
        parts_stored = sem("parts_stored")
        stacks_in = [sem(f"stacks_in{i}") for i in range(NG)]
        kd_ready = sem("kd_ready")
        e_ready = sem("e_ready")
        fixed_ready = sem("fixed_ready")
        s_ready = sem("s_ready")
        r_ready = sem("r_ready")
        rm_ready = sem("rm_ready")
        msplit = sem("msplit")
        mt_ready = sem("mt_ready")
        mt_copied = sem("mt_copied")
        mrows_in = sem("mrows_in")
        st_ready = sem("st_ready")
        exp_ready = sem("exp_ready")
        v_ready = sem("v_ready")
        pv_ready = sem("pv_ready")
        ct_copied = sem("ct_copied")
        vp_ready = sem("vp_ready")
        vp_copied = sem("vp_copied")
        vprep = sem("vprep")
        vact = sem("vact")
        v_mixed = sem("v_mixed")
        c_pe = sem("c_pe")
        c_dve = sem("c_dve")
        c_pool = sem("c_pool")
        c_act = sem("c_act")
        k_dve = sem("k_dve")
        out_done = sem("out_done")
        passed = sem("passed")

        PE_C, DVE_C, POOL_C, ACT_C = 8, 59, 9, 2
        LAG = 6
        MAXIMA_AT = (0, 2)
        CONTEXT_AT = [(3, 0), (3, 2), (4, 0), (5, 3)]
        NORMED_AT, OUTPUT_AT, QUANTIZED_AT, FFN_AT = (6, 2), (7, 1), (13, 3), (14, 1)

        def piece(b, k):
            return 4 * b + (k - 1)

        def hold(eng, s, value):
            if isinstance(value, int):
                if value > 0:
                    eng.wait_ge(s, value)
            else:
                eng.wait_ge(s, value)

        def hold_apart(eng, s, value):
            hold(eng, s, value)
            if not isinstance(value, int):
                eng.sem_inc(passed, 1)

        block = ctx.enter_context(nc.Block())
        NFIRST, NREST, NLATE = 5, 12, 10
        LOADS = 8

        @block.sync
        def _(sp):
            def take(s, dst, src):
                sp.dma_start(dst, src).then_inc(s, 16)

            sp.sem_inc(out_done, 16)
            take(in_first, wqk_sb[:, :, :], wqk)
            take(in_first, hsT_sb[:, 0:S], hsT[:, 0:S])
            take(in_first, bqk_sb[:, :], bqk)
            take(in_first, fac_sb[0][:, :, :], fac_q)
            take(in_first, fac_sb[1][:, :, :], fac_k)
            take(in_rest, wap_sb[:, :], wap)
            take(in_rest, hsT_sb[:, S:B * S], hsT[:, S:B * S])
            take(in_rest, wvn_sb[:, :], wv_nat)
            take(in_rest, mix_sb[:, :], mixbd)
            take(in_rest, wv_sb[:, 0:D], wv)
            take(in_rest, bvc_sb[:, :], bv_col)
            take(in_rest, bap_sb[:, :], bap.partition_broadcast(P))
            take(in_rest, bvv_sb[:, 0:D], bv_row.partition_broadcast(P))
            take(in_rest, bvv_sb[:, D:2 * D], mixb.partition_broadcast(P))
            take(in_rest, km_sb[:, :], kmask)
            take(in_rest, fix_sb[:, :], diagfix)
            take(in_rest, id_sb[:, :], ident)

            def take_late():
                take(in_late, kern_sb[:, :], kern)
                take(in_late, sc_sb[:, 0:1], s_in.partition_broadcast(P))
                take(in_late, sc_sb[:, 1:2], s_k.partition_broadcast(P))
                for h_ in range(2):
                    take(in_late, hs_sb[:, h_ * 8:h_ * 8 + 8, :], hs.rearrange("(i p) d -> p i d", p=P)[:, h_ * 8:h_ * 8 + 8, :])
                take(in_late, wo_sb[:, :], wo)
                take(in_late, bo_sb[:, :], bo.partition_broadcast(P))
                take(in_late, g_sb[:, :], ln_g.partition_broadcast(P))
                take(in_late, b_sb[:, :], ln_b.partition_broadcast(P))
                take(in_late, fb_sb[:, :], fbias.partition_broadcast(P))

            def store(what, b, k, s):
                sp.dma_start(scratch[b, k % 2, k // 2].rearrange("f p r h n -> (r h) (f p) n"),
                             what.rearrange("p f a n -> p (f a) n")).then_inc(s, 16)

            def store_parts(b, k):
                hold_apart(sp, parts_ready, piece(b, k))
                store(parts[:, :, :, :], b, k, parts_stored)

            def load_stacks(b, c):
                bb, g = (b, c) if c < NG else (b + 1, c - NG)
                hold_apart(sp, st_ready, 64 * b + 16 * (c - 3))
                if isinstance(bb, int) and bb == 0 and g < 2:
                    sp.wait_ge(early_stored, 32)
                else:
                    hold_apart(sp, parts_stored, 64 * bb + 32 * (g // 2))
                for row, n in GROUPS:
                    part = 3 - n
                    stack = lambda st_: st_[row:row + n * R, g, :, :, :].rearrange("p f j n -> p f (j n)")
                    from_ = lambda side, p0, p1: scratch[bb, side, g // 2, :, p0:p1, :, 4 * (g % 2):4 * (g % 2) + 4, :]\
                        .rearrange("f p r h n -> (p r) f (h n)")
                    sp.dma_start(stack(Kst), from_(1, 0, n)).then_inc(stacks_in[g], 16)
                    for f in range(2) if n > 1 else ():
                        one = scratch[bb, 0, g // 2, f, part, :, 4 * (g % 2):4 * (g % 2) + 4, :]\
                            .rearrange("r h n -> r (h n)").unsqueeze(0).broadcast_to([n, R, GH * S])
                        sp.dma_start(Qst[row:row + n * R, g, f, :, :].rearrange("p j n -> p (j n)"), one)\
                            .then_inc(stacks_in[g], 16)
                    if n == 1:
                        sp.dma_start(stack(Qst), from_(0, part, part + 1)).then_inc(stacks_in[g], 16)

            for k in range(2):
                sp.wait_ge(early_split, 5 * k + 5)
                store(parts_early[k], 0, k, early_stored)
            load_stacks(0, 0)
            store_parts(0, 2)
            load_stacks(0, 1)
            store_parts(0, 3)
            sp.wait_ge(const_set, 5)
            for g in range(1, NG):
                if g == NG - 1:
                    sp.wait_ge(v_mixed, 5)
                sp.dma_start(Kst[KR:KR + MP, g, :, :, :].rearrange("p f j n -> p (f j n)"),
                             Kst[KR:KR + MP, 0, :, :, :].rearrange("p f j n -> p (f j n)")).then_inc(ones_set, 16)
                if g == 1:
                    load_stacks(0, 2)
                    take_late()

            def write_out(b):
                hold_apart(sp, c_dve, DVE_C * b + DVE_C)
                sp.dma_start(out[b].rearrange("(t p) d -> p t d", p=P), x1[:, :, :]).then_inc(out_done, 16)

            def body(b, first=False, last=False):
                for c in range(NG):
                    if not last:
                        store_parts(b + 1, c)
                    if not last or c == 0:
                        load_stacks(b, c + 3)
                if not first:
                    write_out(b - 1)

            body(0, first=True)
            with sp.Fori(1, B - 1) as b:
                body(b)
            body(B - 1, last=True)
            write_out(B - 1)
            sp.wait_ge(out_done, 16 * B + 16)

        @block.tensor
        def _(pe):
            mm = nc.tensor.matmul

            def project(b, k, wait_sem, wait_value, bank=MB, done=proj_ready):
                hold(pe, wait_sem, wait_value)
                mm(bank[:, :], wqk_sb[:, k, :], hsT_sb[:, bass.ds(b * S, S)] if not isinstance(b, int)
                   else hsT_sb[:, b * S:b * S + S], start=True, stop=True).then_inc(done, 1)

            def entangled(b, c, j):
                g = c % NG
                if j == 0:
                    hold(pe, stacks_in[g], (LOADS * 16) * b + (LOADS * 16) * (1 + c // NG))
                hold(pe, kd_ready, 32 * b + (8 * c + 2 * j + 2))
                hold(pe, fixed_ready, 16 * b + (4 * c + j))
                for t in range(NT):
                    tile = slice(t * P, t * P + P)
                    e = mm(EB[:, tile], Qst[0:KR, g, 0, j, tile], Kd[0:KR, j % 2, 1, tile], start=True, stop=True)
                e.then_inc(e_ready, 1)

            def scores(b, c, j, t):
                g = c % NG
                tile = slice(t * P, t * P + P)
                i = 4 * j + t
                hold(pe, r_ready, 64 * b + (16 * c + (i - 2 if i else 0)))
                bank = SB[i % 3]
                s = mm(bank[:, tile], Qst[0:KR, g, 0, j, tile], Kd[0:KR, j % 2, 0, tile], start=True, stop=True)
                if t > 0:
                    s = mm(bank[:, 0:t * P], Qst[0:KR, g, 0, j, tile], Kst[0:KR, g, 0, j, 0:t * P],
                           start=True, stop=True)
                if t < NT - 1:
                    s = mm(bank[:, (t + 1) * P:S], Qst[0:KR, g, 1, j, tile],
                           Kst[0:KR, g, 1, j, (t + 1) * P:S], start=True, stop=True)
                s.then_inc(s_ready, 1)

            KM = KR + MP

            def scores_t(b, c, t, j):
                g = c % NG
                if t == 0 and j == 0:
                    hold(pe, mrows_in, 128 * b + 32 * (c + 1))
                    if isinstance(b, int) and b == c == 0:
                        pe.wait_ge(ones_set, 16 * (NG - 1))
                        pe.wait_ge(const_set, 5)
                    hold(pe, rm_ready, 16 * b + 4 * (c + 1))
                tile = slice(t * P, t * P + P)
                hold(pe, exp_ready, 64 * b + (16 * c + 4 * t + j - 1))
                bank = ST[j % 2]
                s = mm(bank[:, tile], Rm[:, c % 2, j, t, :], id_sb[:, :], start=True, stop=True, is_transpose=True)
                if t < NT - 1:
                    s = mm(bank[:, (t + 1) * P:S], Kst[0:KM, g, 0, j, tile], Qst[0:KM, g, 0, j, (t + 1) * P:S],
                           start=True, stop=True)
                if t > 0:
                    s = mm(bank[:, 0:t * P], Kst[0:KM, g, 1, j, tile], Qst[0:KM, g, 1, j, 0:t * P],
                           start=True, stop=True)
                s.then_inc(st_ready, 1)

            def contexts(b, c, t):
                if t == 0:
                    hold(pe, v_ready, 4 * b + (c + 1))
                    hold(pe, ct_copied, 4 * b + c)
                hold(pe, exp_ready, 64 * b + (16 * c + 4 * t + 4))
                for j in range(GH):
                    m = mm(CB[32 * j:32 * j + 32, :], Vst[:, c % 2, t, j, :], PT[:, t % 2, j, :],
                           start=(t == 0), stop=(t == NT - 1))
                m.then_inc(pv_ready, 1)

            def maxima_t(b, c, first):
                hold(pe, msplit, 16 * b + 4 * (c + 1))
                if first and c == 0:
                    hold(pe, early_split, 1)
                if not first and c in (1, 2):
                    hold(pe, c_dve, DVE_C * (b - 1) + (6, 9)[c - 1])
                mm(MBh[:, 0:P], mparts[:, :], idb_sb[:, :],
                   start=True, stop=True, is_transpose=True).then_inc(mt_ready, 1)

            def ending(b, slot, i):
                n = lambda x: PE_C * b + x
                after_dve = lambda x: hold(pe, c_dve, DVE_C * b + x)
                if (slot, i) in CONTEXT_AT:
                    t = CONTEXT_AT.index((slot, i))
                    if t == 0:
                        hold(pe, ct_copied, 4 * b + 4)
                    if t > 0:
                        after_dve(2 * t)
                    for g in range(NG):
                        m = mm(MB[:, g * P:g * P + P], CT[:, g, t * P:t * P + P], id_sb[:, :],
                               start=True, stop=True, is_transpose=True)
                    m.then_inc(c_pe, 1)
                if (slot, i) == NORMED_AT:
                    after_dve(8)
                    for t in range(NT):
                        m = mm(MB[:, t * P:t * P + P], cn[:, t, :], id_sb[:, :], start=True, stop=True, is_transpose=True)
                    m.then_inc(c_pe, 1)
                if (slot, i) == OUTPUT_AT:
                    hold(pe, c_act, ACT_C * b + 1)
                    for t in range(NT):
                        m = mm(MB[:, t * P:t * P + P], cnT[:, t * P:t * P + P], wo_sb[:, :], start=True, stop=True)
                    m.then_inc(c_pe, 1)
                if (slot, i) == QUANTIZED_AT:
                    after_dve(44)
                    for t in range(NT):
                        m = mm(MBh[:, t * P:t * P + P], xq[:, t, :], idb_sb[:, :], start=True, stop=True, is_transpose=True)
                    m.then_inc(c_pe, 1)
                if (slot, i) == (15, 3):
                    after_dve(45)
                if (slot, i) == FFN_AT:
                    hold(pe, c_act, ACT_C * b + 2)
                    for t in range(NT):
                        m = mm(MB[:, t * P:t * P + P], xqT[:, t * P:t * P + P], kq_sb[:, :], start=True, stop=True)
                    m.then_inc(c_pe, 1)

            pe.wait_ge(in_first, 16 * NFIRST)
            for k in range(4):
                project(0, k, None, 0, (MB, EB, SB[0], SB[1])[k], early_ready if k < 2 else proj_ready)
            pe.wait_ge(in_rest, 16 * NREST)
            mm(ST[0][:, 0:D], wvn_sb[:, :], mix_sb[:, :], start=True, stop=True)
            pe.wait_ge(vprep, 1)
            mm(ST[0][:, D:2 * D], bvb_sb[:, :], mix_sb[:, :], start=True, stop=True).then_inc(vp_ready, 1)
            for i in range(B * NT):
                m = mm(ST[1][:, i * 2 * H:(i + 1) * 2 * H], hsT_sb[:, i * P:i * P + P], wap_sb[:, :],
                       start=True, stop=True)
            m.then_inc(vp_ready, 1)
            pe.wait_ge(vprep, 3)
            for i in range(B * NT // 2):
                hold(pe, vp_copied, i - 1)
                for h_ in range(2):
                    m = mm(VP[i % 2][:, h_ * 2 * D:(h_ + 1) * 2 * D],
                           hsT_sb[:, (2 * i + h_) * P:(2 * i + h_ + 1) * P], wv_sb[:, :], start=True, stop=True)
                m.then_inc(vp_ready, 1)
            pe.wait_ge(early_split, 6)
            entangled(0, 0, 0)
            pe.wait_ge(proj_copied, 2)
            for j in range(GH):
                for t in range(NT):
                    scores(0, 0, j, t)
                    if j == 0 and t == 1:
                        hold(pe, vp_copied, B * NT // 2)
                    if t == 3:
                        entangled(0, (j + 1) // GH, (j + 1) % GH)
            pe.wait_ge(vprep, 4)
            def step(b, c, t, first, last):
                for i in range(NT):
                    if not (last and c == NG - 1):
                        scores(b, c + 1, t, i)
                    n_ = 4 * (c + 1) + t + 1
                    if i == 3 and not (last and n_ >= H):
                        entangled(b, n_ // 4, n_ % 4)
                    k = 4 * t + i - LAG
                    if not (first and c == 0 and k < 0):
                        scores_t(b, c - (k < 0), k % 16 // 4, k % 4)
                    if i == 0 and not (first and c == 0 and t < 3):
                        contexts(b, c - (t < 3), (t - 3) % NT)
                    if (t, i) == MAXIMA_AT:
                        maxima_t(b, c, first)
                    if (t, i) == (1, 0) and not last:
                        project(b + 1, c, mt_copied, 4 * b + (c + 1))
                    if (t, i) == (1, 3) and not last:
                        hold(pe, proj_copied, piece(b + 1, c))
                    if not first:
                        ending(b - 1, 4 * c + t, i)

            def body(b, first=False, last=False):
                for c in range(NG):
                    for t in range(NT):
                        step(b, c, t, first, last)

            body(0, first=True)
            with pe.Fori(1, B - 1) as b:
                body(b)
            body(B - 1, last=True)
            for k in range(16 - LAG, 16):
                if k == 12:
                    contexts(B - 1, NG - 1, 1)
                scores_t(B - 1, NG - 1, k // 4, k % 4)
            contexts(B - 1, NG - 1, 2)
            contexts(B - 1, NG - 1, 3)
            for slot in range(16):
                for i in range(4):
                    ending(B - 1, slot, i)

        @block.scalar
        def _(act):
            def copy_proj(b, k, bank=MB):
                hold(act, proj_ready, piece(b, k))
                hold(act, faced_ready, piece(b, k) - 1)
                nc.scalar.activation(proj[:, :], bank[:, :], ACT.Identity, bias=bqk_sb[:, k:k + 1])\
                    .then_inc(proj_copied, 1)

            def cast_hi(b, k):
                hold(act, faced_ready, piece(b, k))
                hold(act, parts_stored, 64 * b + 16 * (k - 2))
                nc.scalar.activation(parts[:, :, 0, :], faced[:, :, :], ACT.Copy).then_inc(hi_ready, 1)

            def cast_mid(b, k):
                hold(act, left_ready, piece(b, k))
                nc.scalar.activation(parts[:, :, 1, :], faced[:, :, :], ACT.Copy).then_inc(mid_ready, 1)

            def place_maxima(b, c):
                hold(act, mt_copied, 4 * b + (c + 1))
                for f in range(2):
                    act.dma_start(Qst[KR:KR + MP, c, f, :, :].rearrange("p j n -> p (j n)"), mrows[:, :])\
                        .then_inc(mrows_in, 16)

            def exps(b, c, t, j):
                if j == 0:
                    hold(act, pv_ready, 16 * b + (4 * c + t - 1))
                hold(act, st_ready, 64 * b + (16 * c + 4 * t + j + 1))
                nc.scalar.activation(PT[:, t % 2, j, :], ST[j % 2][:, :], ACT.Exp).then_inc(exp_ready, 1)

            def copy_contexts(b, c):
                hold(act, pv_ready, 16 * b + 4 * (c + 1))
                if c == 0:
                    hold(act, c_pe, PE_C * b - 4)
                nc.scalar.activation(CT[:, c % NG, :], CB[:, :], ACT.Copy).then_inc(ct_copied, 1)

            def ending(b, slot):
                if slot == 7:
                    hold(act, c_pe, PE_C * b + 5)
                    nc.scalar.activation(cnT[:, :], MB[:, :], ACT.Copy).then_inc(c_act, 1)
                if slot == 14:
                    hold(act, c_pe, PE_C * b + 7)
                    nc.scalar.activation(xqT[:, :], MBh[:, 0:S], ACT.Copy).then_inc(c_act, 1)

            act.wait_ge(in_first, 16 * NFIRST)
            copy_proj(0, 2, SB[0])
            cast_hi(0, 2)
            copy_proj(0, 3, SB[1])
            cast_mid(0, 2)
            cast_hi(0, 3)
            cast_mid(0, 3)
            act.wait_ge(vprep, 4)
            co = lambda i: co_sb[:, i, :].rearrange("p (i h) -> p i h", h=H)
            nc.scalar.activation(co(0), ap_sb[:, :, 0:H], ACT.Exp, scale=-1.0).then_inc(vact, 1)
            nc.scalar.activation(co(1), ap_sb[:, :, H:2 * H], ACT.Tanh).then_inc(vact, 1)
            act.wait_ge(vact, 2)
            nc.scalar.activation(co_sb[:, 2, :], co_sb[:, 1, :], ACT.Sin, scale=math.pi).then_inc(vact, 1)
            act.wait_ge(const_set, 2)
            act.wait_ge(vprep, 5)
            nc.scalar.activation(co_sb[:, 3, :], co_sb[:, 3, :], ACT.Sin, scale=-math.pi, bias=halfpi[:, :])\
                .then_inc(vact, 1)

            def body(b, first=False, last=False):
                for c in range(NG):
                    for t in range(NT):
                        if not first:
                            ending(b - 1, 4 * c + t)
                        for j in range(GH):
                            k = 4 * t + j - LAG
                            if not (first and c == 0 and k < 0):
                                exps(b, c - (k < 0), k % 16 // 4, k % 4)
                            if (t, j) == (2, 1) and not (first and c == 0):
                                copy_contexts(b, c - 1)
                            if (t, j) == (0, 2):
                                place_maxima(b, c)
                            if not last and (t, j) == (1, 0):
                                copy_proj(b + 1, c)
                            if not last and (t, j) == (2, 0):
                                cast_hi(b + 1, c)
                            if not last and (t, j) == (3, 0):
                                cast_mid(b + 1, c)

            body(0, first=True)
            with act.Fori(1, B - 1) as b:
                body(b)
            body(B - 1, last=True)
            for k in range(16 - LAG, 16):
                exps(B - 1, NG - 1, k // 4, k % 4)
            copy_contexts(B - 1, NG - 1)
            for slot in range(16):
                ending(B - 1, slot)

        @block.gpsimd
        def _(pool):
            pool.memset(neghalf[:, :], -0.5).then_inc(const_set, 1)
            pool.memset(halfpi[:, :], math.pi / 2).then_inc(const_set, 1)
            pool.memset(Vst[:, :, :, :, :], 0.0).then_inc(const_set, 1)
            pool.wait_ge(const_set, 3)
            pool.memset(Vst[:, :, :, :, HD:HD + 1], 1.0).then_inc(const_set, 1)
            pool.wait_ge(const_set, 4)
            pool.memset(Kst[KR:KR + MP, 0, :, :, :], 1.0).then_inc(const_set, 1)
            pool.wait_ge(in_first, 16 * NFIRST)
            pool.wait_ge(const_set, 5)

            def split(b, k, step):
              if step == 0:
                hold(pool, proj_copied, piece(b, k))
                hold(pool, parts_ready, piece(b, k) - 1)
                both = proj[:, :].unsqueeze(1).broadcast_to([P, 2, S])
                nc.gpsimd.tensor_tensor(faced[:, :, :], both, fac_sb[k % 2][:, :, :], ALU.mult)\
                    .then_inc(faced_ready, 1)
              if step == 1:
                hold(pool, hi_ready, piece(b, k))
                nc.gpsimd.tensor_tensor(faced[:, :, :], faced[:, :, :], parts[:, :, 0, :], ALU.subtract)\
                    .then_inc(left_ready, 1)
              if step == 2:
                hold(pool, mid_ready, piece(b, k))
                nc.gpsimd.tensor_tensor(parts[:, :, 2, :], faced[:, :, :], parts[:, :, 1, :], ALU.subtract)\
                    .then_inc(parts_ready, 1)

            def less_maxima(b, c, j):
                g = c % NG
                hold(pool, r_ready, 16 * (4 * b) + (16 * c + 4 * j + 4))
                hold(pool, st_ready, 16 * (4 * b) + 16 * (c - 1))
                m = mx[:, g % 2, NT * j:NT * j + NT].unsqueeze(2).broadcast_to([P, NT, P])
                nc.gpsimd.tensor_tensor(Rm[:, g % 2, j, :, :], scored_diag[j % 2], m, ALU.subtract).then_inc(rm_ready, 1)

            def place_values(b, c):
                hold_apart(pool, pv_ready, 16 * b + 4 * (c - 1))
                if isinstance(b, int):
                    src = V[:, b * NT:b * NT + NT, c * GH:c * GH + GH, :]
                else:
                    src = V[:, bass.ds(b * NT, NT), c * GH:c * GH + GH, :]
                pool.tensor_copy(Vst[:, c % 2, :, :, 0:HD], src).then_inc(v_ready, 1)

            def ending(b, slot):
                def reciprocal_root(before, n):
                    hold_apart(pool, c_dve, DVE_C * b + before)
                    pool.tensor_scalar(ve[:, :], mv[:, :, 1], EPS, None, ALU.add).then_inc(c_pool, 1)
                    hold(pool, c_pool, POOL_C * b + n)
                    nc.gpsimd.tensor_tensor(rstd[:, :], ve[:, :], neghalf[:, :], ALU.pow).then_inc(c_pool, 1)

                rows = lambda x: x[:, :].unsqueeze(1).broadcast_to([P, NT, D])
                if slot == 8:
                    reciprocal_root(18, 1)
                if slot == 10:
                    hold(pool, c_dve, DVE_C * b + 22)
                    nc.gpsimd.tensor_tensor(x1[:, :, :], x1[:, :, :], rows(g_sb), ALU.mult).then_inc(c_pool, 1)
                    hold(pool, c_pool, POOL_C * b + 3)
                    nc.gpsimd.tensor_tensor(x1[:, :, :], x1[:, :, :], rows(b_sb), ALU.add).then_inc(c_pool, 1)
                    hold_apart(pool, c_pool, POOL_C * b + 4)
                    h_ = hs_sb[:, b * NT:b * NT + NT, :] if isinstance(b, int) else hs_sb[:, bass.ds(b * NT, NT), :]
                    nc.gpsimd.tensor_tensor(x1[:, :, :], x1[:, :, :], h_, ALU.add).then_inc(c_pool, 1)
                if slot == 11:
                    reciprocal_root(30, 6)
                if slot == 15:
                    reciprocal_root(55, 8)

            for k in (2, 3):
                for step in range(3):
                    split(0, k, step)
            def mix(half, stage):
                tiles = slice(half * HALF, (half + 1) * HALF)
                sup = VS[half][:, :, D:2 * D].rearrange("p i (h d) -> p i h d", d=HD)
                val = VS[half][:, :, 0:D].rearrange("p i (h d) -> p i h d", d=HD)
                dst = V[:, tiles, :, :]
                fac = lambda i, n: co_sb[:, i, :].rearrange("p (i h) -> p i h", h=H)[:, tiles, :].unsqueeze(3)\
                    .broadcast_to([P, HALF, H, n])
                tt = nc.gpsimd.tensor_tensor
                if stage == 0:
                    if half:
                        pool.wait_ge(v_mixed, 5 * half)
                    tt(dst, sup, fac(3, HD), ALU.mult).then_inc(v_mixed, 1)
                    pool.wait_ge(v_mixed, 5 * half + 1)
                    tt(val, val, dst, ALU.add).then_inc(v_mixed, 1)
                if stage == 1:
                    pool.wait_ge(v_mixed, 5 * half + 2)
                    tt(dst[:, :, :, 1:HD], sup[:, :, :, 0:HD - 1], fac(2, HD - 1), ALU.mult).then_inc(v_mixed, 1)
                    tt(dst[:, :, :, 0:1], sup[:, :, :, HD - 1:HD], fac(2, 1), ALU.mult).then_inc(v_mixed, 1)
                    pool.wait_ge(v_mixed, 5 * half + 4)
                    tt(dst, val, dst, ALU.add).then_inc(v_mixed, 1)

            pool.wait_ge(vprep, 10)
            for j in range(GH):
                mix(j // 2, j % 2)
                less_maxima(0, 0, j)
            pool.wait_ge(v_mixed, 10)

            def body(b, first=False, last=False):
                for c in range(NG):
                    for j in range(GH):
                        if not first:
                            ending(b - 1, 4 * c + j)
                        if j == 0:
                            place_values(b, c)
                            if not last:
                                split(b + 1, c, 0)
                        if not (last and c == NG - 1):
                            less_maxima(b, c + 1, j)
                        if j in (1, 2) and not last:
                            split(b + 1, c, j)

            body(0, first=True)
            with pool.Fori(1, B - 1) as b:
                body(b)
            body(B - 1, last=True)
            for slot in range(16):
                ending(B - 1, slot)

        @block.vector
        def _(dve):
            v = nc.vector
            bc = lambda x, n=NT: x[:, :].unsqueeze(1).broadcast_to([P, n, D])
            v.memset(fixed_all[:, :], 0.0).then_inc(k_dve, 1)
            v.memset(mparts[:, :], 0.0).then_inc(k_dve, 1)
            dve.wait_ge(in_first, 16 * NFIRST)
            n_early = [0]

            def early(ins):
                n_early[0] += 1
                ins.then_inc(early_split, 1)
                dve.wait_ge(early_split, n_early[0])

            for k, bank in ((0, MB), (1, EB)):
                dve.wait_ge(early_ready, k + 1)
                early(v.scalar_tensor_tensor(out=faced_early, in0=bank[:, :].unsqueeze(1).broadcast_to([P, 2, S]),
                                             scalar=bqk_sb[:, k:k + 1], in1=fac_sb[k][:, :, :],
                                             op0=ALU.add, op1=ALU.mult))
                part = lambda i: parts_early[k][:, :, i, :]
                early(v.tensor_copy(part(0), faced_early))
                early(v.tensor_tensor(faced_early, faced_early, part(0), ALU.subtract))
                early(v.tensor_copy(part(1), faced_early))
                early(v.tensor_tensor(part(2), faced_early, part(1), ALU.subtract))
            dve.wait_ge(in_rest, 16 * NREST)
            v.tensor_copy(bvb_sb[:, :], bvc_sb[:, 0:1].broadcast_to([P, P])).then_inc(vprep, 1)
            dve.wait_ge(vp_ready, 1)
            v.tensor_copy(wv_sb[:, D:2 * D], ST[0][:, 0:D]).then_inc(vprep, 1)
            v.tensor_tensor(bvv_sb[:, D:2 * D], bvv_sb[:, D:2 * D], ST[0][:, D:2 * D], ALU.add).then_inc(vprep, 1)
            dve.wait_ge(vp_ready, 2)
            v.tensor_tensor(ap_sb[:, :, :], ST[1][:, :].rearrange("p (i n) -> p i n", n=2 * H),
                            bap_sb[:, :].unsqueeze(1).broadcast_to([P, B * NT, 2 * H]), ALU.add).then_inc(vprep, 1)
            dve.wait_ge(vprep, 4)
            for i in range(B * NT // 2):
                dve.wait_ge(vp_ready, 3 + i)
                v.tensor_tensor(VS[2 * i // HALF][:, 2 * i % HALF:2 * i % HALF + 2, :], VP[i % 2][:, :].rearrange("p (i n) -> p i n", i=2),
                                bvv_sb[:, :].unsqueeze(1).broadcast_to([P, 2, 2 * D]), ALU.add).then_inc(vp_copied, 1)
            dve.wait_ge(vact, 3)
            chain = [5]

            def link(ins):
                chain[0] += 1
                ins.then_inc(vprep, 1)
                dve.wait_ge(vprep, chain[0])

            v.tensor_scalar(co_sb[:, 3, :].bitcast(u32), co_sb[:, 1, :].bitcast(u32), 0x7FFFFFFF, None, ALU.bitwise_and).then_inc(vprep, 1)
            dve.wait_ge(vprep, 5)
            link(v.tensor_scalar(co_sb[:, 0, :], co_sb[:, 0, :], 1.0, None, ALU.add))
            link(v.reciprocal(co_sb[:, 0, :], co_sb[:, 0, :]))
            link(v.tensor_scalar(co_sb[:, 0, :], co_sb[:, 0, :], SUP, None, ALU.mult))
            dve.wait_ge(vact, 4)
            dve.wait_ge(vp_copied, B * NT // 2)
            v.tensor_tensor(co_sb[:, 3, :], co_sb[:, 3, :], co_sb[:, 0, :], ALU.mult).then_inc(vprep, 1)
            v.tensor_tensor(co_sb[:, 2, :], co_sb[:, 2, :], co_sb[:, 0, :], ALU.mult).then_inc(vprep, 1)
            kk = [2]

            def klink(ins):
                kk[0] += 1
                ins.then_inc(k_dve, 1)
                dve.wait_ge(k_dve, kk[0])

            klink(v.tensor_copy(idb_sb[:, :], id_sb[:, :]))
            def quantize(dst, src, a, t1, t2, scale, step, part=(0, 9), n=None, base=0, settle=None):
                if n is not None and part[0] > 0:
                    n[0] = base + part[0]
                    settle()
                bits = lambda x: x.bitcast(u32)
                for k in range(*part):
                    if k == 0:
                        step(v.tensor_scalar(a, src, scale, None, ALU.mult))
                    if k == 1:
                        step(v.tensor_scalar(bits(t1), bits(a), 0x7F800000, None, ALU.bitwise_and))
                    if k == 2:
                        step(v.tensor_scalar(t1, t1, 2.0 ** -6, 1.5 * 2.0 ** 20, ALU.max, ALU.mult))
                    if k == 3:
                        step(v.tensor_tensor(a, a, t1, ALU.add))
                    if k == 4:
                        step(v.tensor_tensor(a, a, t1, ALU.subtract))
                    if k == 5:
                        step(v.tensor_tensor(t1, a, a, ALU.mult))
                    if k == 6:
                        step(v.tensor_scalar(t1, t1, 448.0 ** 2, 3e38, ALU.is_gt, ALU.mult))
                    if k == 7:
                        step(v.tensor_scalar(t1, t1, 3e38, 0.0, ALU.mult, ALU.mult))
                    if k == 8:
                        step(v.tensor_tensor(dst, a, t1, ALU.add))

            QUANTIZE_AT = ((0, 2), (2, 5), (5, 7), (7, 9))

            def quantize_kernel():
                dve.wait_ge(in_late, 16 * NLATE)
                klink(v.reciprocal(rs_sb[:, :], sc_sb[:, :]))
                klink(v.tensor_tensor(ss_sb[:, :], sc_sb[:, 0:1], sc_sb[:, 1:2], ALU.mult))
                quantize(kq_sb[:, :], kern_sb[:, :], q1[:, 0, :], q2[:, 0, :], None, rs_sb[:, 1:2], klink)

            def k_stacks(b, c, j):
                g = c % NG
                if j == 0:
                    hold(dve, stacks_in[g], (LOADS * 16) * b + (LOADS * 16) * (1 + c // NG))
                hold(dve, s_ready, 64 * b + (16 * c + 4 * j - 4))
                for s in range(2):
                    v.tensor_scalar(Kd[0:KR, j % 2, s, :], Kst[0:KR, g, 0, j, :], km_sb[0:KR, s:s + 1], None, ALU.mult)\
                        .then_inc(kd_ready, 1)

            def fix_diagonal(b, c, j):
                hold(dve, e_ready, 16 * b + (4 * c + j + 1))
                hold(dve, r_ready, 64 * b + (16 * c + 4 * j))
                v.tensor_tensor(fixed_diag, EB[:, :].rearrange("p (t n) -> p t n", t=NT), bc(fix_sb), ALU.mult)\
                    .then_inc(fixed_ready, 1)

            def complete(b, c, j, t):
                g = c % NG
                hold_apart(dve, s_ready, 64 * b + (16 * c + 4 * j + t + 1))
                if t == 0:
                    hold_apart(dve, fixed_ready, 16 * b + (4 * c + j + 1))
                    hold_apart(dve, rm_ready, 16 * b + (4 * c + j - 1))
                v.tensor_tensor_reduce(out=scored[j % 2][:, t, :], in0=SB[(4 * j + t) % 3][:, :], in1=fixed[:, t, :], scale=1.0,
                                       scalar=NEG, op0=ALU.add, op1=ALU.max,
                                       accum_out=mx[:, g % 2, NT * j + t:NT * j + t + 1]).then_inc(r_ready, 1)

            def split_maxima(b, c):
                g = c % NG
                m = mx[:, g % 2, :]
                x = lambda k: 16 * b + (4 * c + k)
                hold(dve, r_ready, 64 * b + (16 * c + 16))
                hold(dve, mt_ready, 4 * b + c)
                v.tensor_scalar(mpart(0), m, -1.0, None, ALU.mult).then_inc(msplit, 1)
                hold(dve, msplit, x(1))
                v.scalar_tensor_tensor(out=mneg[:, :], in0=m, scalar=-1.0, in1=mpart(0),
                                       op0=ALU.mult, op1=ALU.subtract).then_inc(msplit, 1)
                hold(dve, msplit, x(2))
                v.tensor_copy(mpart(1), mneg[:, :]).then_inc(msplit, 1)
                hold(dve, msplit, x(3))
                v.tensor_tensor(mpart(2), mneg[:, :], mpart(1), ALU.subtract).then_inc(msplit, 1)

            def copy_maxima(b, c):
                hold(dve, mt_ready, 4 * b + (c + 1))
                hold(dve, mrows_in, 128 * b + 32 * c)
                v.tensor_copy(mrows[:, :], MBh[0:MP * GH * NT, 0:P]).then_inc(mt_copied, 1)

            def ending(b, slot, i):
                n = [0]
                done = lambda x: DVE_C * b + x

                def step(ins, chained=True):
                    n[0] += 1
                    ins.then_inc(c_dve, 1)
                    if chained:
                        settle()

                def settle():
                    hold_apart(dve, c_dve, done(n[0]))

                def stats(x, at):
                    n[0] = at
                    settle()
                    for t in range(NT):
                        step(v.bn_stats(st[:, t, :], x[:, t, :]), False)

                def aggregate(at):
                    n[0] = at
                    settle()
                    for t in range(NT):
                        step(v.bn_aggr(mv[:, t, :], st[:, t, :]), False)

                def normalize(dst, x, at, ready):
                    n[0] = at
                    settle()
                    hold_apart(dve, c_pool, POOL_C * b + ready)
                    for t in range(NT):
                        step(v.tensor_scalar(dst[:, t, :], x[:, t, :], mv[:, t, 0:1], rstd[:, t:t + 1],
                                             ALU.subtract, ALU.mult), False)

                product = MB[:, :].rearrange("p (t n) -> p t n", t=NT)
                here = (slot, i)
                if here in ((3, 1), (3, 3), (4, 0), (6, 0)):
                    t = ((3, 1), (3, 3), (4, 0), (6, 0)).index(here)
                    hold(dve, c_pe, PE_C * b + t + 1)
                    parts_ = MB[:, :].rearrange("p (h n) -> p h n", n=32)
                    n[0] = 2 * t
                    v.reciprocal(rden[:, t, :], parts_[:, :, HD]).then_inc(c_dve, 1)
                    n[0] += 1
                    hold(dve, c_dve, done(n[0]))
                    step(v.tensor_tensor(cn[:, t, :].rearrange("p (h d) -> p h d", d=HD), parts_[:, :, 0:HD],
                                         rden[:, t, :].unsqueeze(2).broadcast_to([P, H, HD]), ALU.mult), False)
                if here == (7, 3):
                    hold(dve, c_pe, PE_C * b + 6)
                    hold(dve, out_done, 16 * b + 16)
                    n[0] = 8
                    step(v.tensor_tensor(x1[:, :, :], product, bc(bo_sb), ALU.add))
                    h_ = hs_sb[:, b * NT:b * NT + NT, :] if isinstance(b, int) else hs_sb[:, bass.ds(b * NT, NT), :]
                    step(v.tensor_tensor(x1[:, :, :], x1[:, :, :], h_, ALU.add), False)
                if here == (8, 1):
                    stats(x1, 10)
                if here == (8, 2):
                    aggregate(14)
                if here == (9, 1):
                    normalize(x1, x1, 18, 2)
                if here == (11, 0):
                    hold_apart(dve, c_pool, POOL_C * b + 5)
                    stats(x1, 22)
                if here == (11, 1):
                    aggregate(26)
                if here == (11, 3):
                    normalize(x2, x1, 30, 7)
                if slot == 12:
                    if i == 0:
                        n[0] = 34
                        settle()
                        step(v.tensor_copy(xb[:, :, :], x2[:, :, :]))
                    quantize(xq[:, :, :], xb[:, :, :], q1[:, :, :], q2[:, :, :], None, rs_sb[:, 0:1], step,
                             QUANTIZE_AT[i], n, 35, settle)
                if here == (14, 3):
                    hold(dve, c_pe, PE_C * b + PE_C)
                    n[0] = 44
                    step(v.tensor_scalar(xb[:, :, :], product, ss_sb[:, 0:1], None, ALU.mult))
                    step(v.tensor_tensor(xb[:, :, :], xb[:, :, :], bc(fb_sb), ALU.add))
                    step(v.tensor_tensor(x2[:, :, :], x2[:, :, :], xb[:, :, :], ALU.add), False)
                if here == (15, 0):
                    stats(x2, 47)
                if here == (15, 1):
                    aggregate(51)
                if here == (15, 3):
                    normalize(x1, x2, 55, 9)

            k_stacks(0, 0, 0)
            for j in range(GH):
                fix_diagonal(0, 0, j)
                for t in range(NT):
                    complete(0, 0, j, t)
                    if t == 1:
                        k_stacks(0, (j + 1) // GH, (j + 1) % GH)
            split_maxima(0, 0)

            def body(b, first=False, last=False):
                for c in range(NG):
                    more = not (last and c == NG - 1)
                    for j in range(GH):
                        n_ = 4 * (c + 1) + j + 1
                        if more:
                            fix_diagonal(b, c + 1, j)
                        for t in range(NT):
                            if more:
                                complete(b, c + 1, j, t)
                            if j == 0 and t == 1:
                                copy_maxima(b, c)
                            if t == 1 and not (last and n_ >= H):
                                k_stacks(b, n_ // 4, n_ % 4)
                            if not first:
                                ending(b - 1, 4 * c + j, t)
                    if more:
                        split_maxima(b, c + 1)
                    if first and c == 0:
                        quantize_kernel()

            body(0, first=True)
            with dve.Fori(1, B - 1) as b:
                body(b)
            body(B - 1, last=True)
            for slot in range(16):
                for i in range(4):
                    ending(B - 1, slot, i)


def _constants(np):
    pos = np.arange(S) - (S - 1) / 2
    far = np.exp(-DECAY * pos)
    fac_q, fac_k = np.ones((2, P, 2, S))
    fac_q[:HD * CH] = SCALE
    fac_q[HD * CH:, 0], fac_q[HD * CH:, 1] = ENT * SCALE * far, ENT * SCALE / far
    fac_k[HD * CH:, 0], fac_k[HD * CH:, 1] = 1 / far, far
    q, k = np.arange(P)[:, None], np.arange(P)[None, :]
    diagfix = np.where(q >= k, 1.0, np.exp(-2 * DECAY * (k - q)))
    kmask = np.zeros((P, 2))
    for row, n in GROUPS:
        for i in range(n * R):
            kmask[row + i, i % R // HD] = 1
    return {"fac_q": fac_q, "fac_k": fac_k, "ident": np.eye(P), "diagfix": diagfix, "kmask": kmask}


def kernel(**inputs):
    import numpy as np
    import concourse.bacc as _bacc
    from concourse.bass_utils import run_bass_kernel_spmd as _run

    a = {n.removeprefix("L0_"): np.asarray(x) for n, x in inputs.items()}
    w = {n.removeprefix("attn_"): x for n, x in a.items()}
    f32 = np.float32
    tokens = w["hidden_states"].reshape(B * S, D)

    def chunked(x, kind):
        return x.reshape(H // CH, CH, HD, *x.shape[1:]).swapaxes(1, 2)

    def rows(plain, entangled):
        x = np.concatenate([chunked(plain, 0), chunked(entangled, 1)], axis=1)
        return x.reshape(H // CH, P, *x.shape[3:])

    wq, wk = rows(w["Wq"], w["Weq"]), rows(w["Wk"], w["Wek"])
    bq, bk = rows(w["bq"], w["beq"]), rows(w["bk"], w["bek"])
    mixbd = np.zeros((H, HD, H, HD), f32)
    for h in range(H):
        mixbd[h, :, h, :] = w["mix_w"][h].T
    arrays = {
        "hs": tokens, "hsT": tokens.T,
        "wqk": np.stack([wq[0], wk[0], wq[1], wk[1]]).transpose(2, 0, 1),
        "bqk": np.stack([bq[0], bk[0], bq[1], bk[1]]).T,
        "wv": w["Wv"].T, "wv_nat": w["Wv"], "mixbd": mixbd.reshape(D, D), "bv_col": w["bv"].reshape(D, 1),
        "mixb": w["mix_b"].reshape(D), "wap": np.concatenate([w["amp_w"], w["ph_w"]]).T,
        "bap": np.concatenate([w["amp_b"], w["ph_b"]]), "bv_row": w["bv"], "wo": w["Wo"].T, "bo": w["bo"],
        "ln_g": w["ln_g"], "ln_b": w["ln_b"], "kern": w["ffn_kernel"], "s_in": w["ffn_input_scale"],
        "s_k": w["ffn_kernel_scale"], "fbias": w["ffn_bias"],
    }
    arrays.update({n: x.astype(f32) for n, x in _constants(np).items()})
    arrays = {f"in_{n}": np.ascontiguousarray(x) for n, x in arrays.items()}

    nc = _bacc.Bacc("TRN2", target_bir_lowering=False, num_devices=1)
    args = {n.removeprefix("in_"): nc.dram_tensor(n, x.shape, mybir.dt.from_np(x.dtype), kind="ExternalInput").ap()
            for n, x in arrays.items()}
    scratch = nc.dram_tensor("stacks", (B, 2, H // CH, 2, 3, R, CH, S), bf16, kind="Internal").ap()
    out = nc.dram_tensor("out", (B, S, D), fp32, kind="ExternalOutput").ap()
    attention_block(nc, scratch=scratch, out=out, **args)
    r = _run(nc, [arrays], core_ids=[0])
    return r.results[0]["out"]
```

```python
import concourse.bass as bass
from concourse import mybir
from contextlib import ExitStack
import math

fp32 = mybir.dt.float32
bf16 = mybir.dt.bfloat16
u32 = mybir.dt.uint32
ALU = mybir.AluOpType
ACT = mybir.ActivationFunctionType

B, S, D, H = 4, 512, 128, 16
HD = D // H
P = 128
NT = S // P
GH = 4
NG = H // GH
CH = 8
R = 2 * HD
TERMS = 6
KR = TERMS * R
MP = 3
SUP, DECAY, ENT, EPS = 0.3, 0.1, 0.5, 1e-5
SCALE = 1.0 / math.sqrt(HD)
NEG = -3.0e38
GROUPS = ((0, 3), (3 * R, 2), (5 * R, 1))


def attention_block(nc, hs, hsT, wqk, bqk, fac_q, fac_k, wv, wv_nat, mixbd, bv_col, mixb, wap, bap,
                    bv_row, wo, bo, ln_g, ln_b, kern, s_in, s_k, fbias, ident, diagfix, kmask,
                    scratch, out):
    ctx = ExitStack()
    with ctx:
        def sb(name, shape, dt=fp32):
            return ctx.enter_context(nc.sbuf_tensor(name, shape, dt))

        def pb(name):
            return ctx.enter_context(nc.psum_tensor(name, [P, 512], fp32))

        def sem(name):
            return ctx.enter_context(nc.semaphore(name))

        hsT_sb = sb("hsT_sb", [P, B * S])
        hs_sb = sb("hs_sb", [P, B * NT, D])
        wqk_sb = sb("wqk_sb", [P, 4, P])
        bqk_sb = sb("bqk_sb", [P, 4])
        fac_sb = [sb("facq_sb", [P, 2, S]), sb("fack_sb", [P, 2, S])]
        bvc_sb = sb("bvc_sb", [P, 1])
        wap_sb = sb("wap_sb", [P, 2 * H])
        bap_sb = sb("bap_sb", [P, 2 * H])
        wo_sb = sb("wo_sb", [P, D])
        bo_sb = sb("bo_sb", [P, D])
        g_sb = sb("g_sb", [P, D])
        b_sb = sb("b_sb", [P, D])
        kern_sb = sb("kern_sb", [P, D], bf16)
        kq_sb = sb("kq_sb", [P, D], bf16)
        sc_sb = sb("sc_sb", [P, 2])
        rs_sb = sb("rs_sb", [P, 2])
        ss_sb = sb("ss_sb", [P, 1])
        fb_sb = sb("fb_sb", [P, D], bf16)
        id_sb = sb("id_sb", [P, P])
        idb_sb = sb("idb_sb", [P, P], bf16)
        fix_sb = sb("fix_sb", [P, P])
        km_sb = sb("km_sb", [P, 2])
        neghalf = sb("neghalf", [P, NT])
        halfpi = sb("halfpi", [P, 1])

        proj = sb("proj", [P, S])
        faced = sb("faced", [P, 2, S])
        parts = sb("parts", [P, 2, 3, S], bf16)

        Qst = sb("Qst", [P, NG, 2, GH, S], bf16)
        Kst = sb("Kst", [P, NG, 2, GH, S], bf16)
        Kd = sb("Kd", [P, 2, 2, S], bf16)
        fixed_all = sb("fixed", [P, NT * (S + P)])
        R_all = sb("R_sb", [P, 2, NT * (S + P)])
        Rm = sb("Rm", [P, 2, GH, NT, P])
        mx = sb("mx", [P, 2, GH * NT])
        mneg = sb("mneg", [P, GH * NT])
        mparts = sb("mparts", [P, P], bf16)
        mrows = sb("mrows", [MP * GH * NT, P], bf16)
        PT = sb("PT", [P, 2, GH, S])
        V = sb("V", [P, B * NT, H, HD])
        Vst = sb("Vst", [P, 2, NT, GH, 32])
        CT = sb("CT", [P, 2, S])

        by_tile = lambda x: x[:, 0:NT * S].rearrange("p (t n) -> p t n", t=NT)
        on_diagonal = lambda x: x[:, :].rearrange("p (t n) -> p t n", t=NT)[:, :, 0:P]
        fixed, fixed_diag = by_tile(fixed_all), on_diagonal(fixed_all)
        scored = [by_tile(R_all[:, i, :]) for i in range(2)]
        scored_diag = [on_diagonal(R_all[:, i, :]) for i in range(2)]
        mpart = lambda i: mparts[:, i * GH * NT:(i + 1) * GH * NT]

        R_flat = R_all[:, :, :].rearrange("p a b -> p (a b)")
        faced_early = R_flat[:, 0:2 * S].rearrange("p (f n) -> p f n", f=2)
        parts_early = [R_flat[:, (2 + 3 * i) * S:(5 + 3 * i) * S].bitcast(bf16).rearrange("p (f a n) -> p f a n", f=2, a=3)
                       for i in range(2)]

        early = PT[:, :, :, :].rearrange("p a b c -> p (a b c)")
        at = [0]

        def lent(n):
            at[0] += n
            return early[:, at[0] - n:at[0]]

        wv_sb = lent(2 * D)
        wvn_sb, mix_sb, bvb_sb = lent(D), lent(D), lent(P)
        bvv_sb = lent(2 * D)
        ap_sb = lent(B * NT * 2 * H).rearrange("p (i n) -> p i n", n=2 * H)
        co_sb = lent(4 * B * NT * H).rearrange("p (k n) -> p k n", k=4)
        rden = sb("rden", [P, NT, GH])
        cn = sb("cn", [P, NT, D])
        hs_bo = sb("hs_bo", [P, NT, D])
        hs_b = sb("hs_b", [P, NT, D])
        x1 = sb("x1", [P, NT, D])
        x2 = sb("x2", [P, NT, D])
        st = sb("st", [P, NT, 6])
        mv = sb("mv", [P, NT, 2])
        ve = sb("ve", [P, NT])
        rstd = sb("rstd", [P, NT])
        q1 = sb("q1", [P, NT, D])
        q2 = sb("q2", [P, NT, D])
        cnT = q2[:, :, :].rearrange("p t n -> p (t n)")
        xb = sb("xb", [P, NT, D], bf16)
        xq = sb("xq", [P, NT, D], bf16)
        xqT = sb("xqT", [P, S], bf16)

        factor = {i: x[:, 2:4, :].rearrange("p t n -> p (t n)") for i, x in ((3, q1), (2, q2))}
        VS = [Qst[:, NG - 1, :, :, :].rearrange("p f j n -> p (f j n)").bitcast(fp32)
              .rearrange("p (i n) -> p i n", n=2 * D)]
        VS += [x[:, :, :].rearrange("p t n -> p (t n)").rearrange("p (i n) -> p i n", n=2 * D)
               for x in (x1, x2, hs_bo, hs_b)]
        HALF = B * NT // 2

        SB = [pb(f"SB{i}") for i in range(3)]
        EB = pb("EB")
        ST = [pb("ST0"), pb("ST1")]
        CB = pb("CB")
        MB = pb("MB")
        VP = [CB, ST[1]]
        MBh = MB[:, :].bitcast(bf16)

        in_first = sem("in_first")
        in_rest = sem("in_rest")
        in_late = sem("in_late")
        ones_set = sem("ones_set")
        early_ready = sem("early_ready")
        early_split = sem("early_split")
        early_stored = sem("early_stored")
        const_set = sem("const_set")
        proj_ready = sem("proj_ready")
        proj_copied = sem("proj_copied")
        faced_ready = sem("faced_ready")
        hi_ready = sem("hi_ready")
        left_ready = sem("left_ready")
        mid_ready = sem("mid_ready")
        parts_ready = sem("parts_ready")
        parts_stored = sem("parts_stored")
        stacks_in = [sem(f"stacks_in{i}") for i in range(NG)]
        ek_alone_ready = sem("ek_alone_ready")
        e_ready = sem("e_ready")
        fixed_ready = sem("fixed_ready")
        s_ready = sem("s_ready")
        r_ready = sem("r_ready")
        rm_ready = sem("rm_ready")
        msplit = sem("msplit")
        mt_ready = sem("mt_ready")
        mt_copied = sem("mt_copied")
        mrows_in = sem("mrows_in")
        st_ready = sem("st_ready")
        exp_ready = sem("exp_ready")
        v_ready = sem("v_ready")
        pv_ready = sem("pv_ready")
        ct_copied = sem("ct_copied")
        vp_ready = sem("vp_ready")
        vp_copied = sem("vp_copied")
        vprep = sem("vprep")
        vact = sem("vact")
        v_mixed = sem("v_mixed")
        ctx_turned = sem("ctx_turned")
        ctx_normed = sem("ctx_normed")
        k_alone_ready = sem("k_alone_ready")
        c_pe = sem("c_pe")
        c_dve = sem("c_dve")
        c_pool = sem("c_pool")
        c_act = sem("c_act")
        k_dve = sem("k_dve")
        out_done = sem("out_done")
        passed = sem("passed")

        LAG = 8
        MAXIMA_AT = (0, 1)
        PE_C, DVE_C, POOL_C, ACT_C = 4, 47, 10, 5
        NORMED_AT, OUTPUT_AT, QUANTIZED_AT, FFN_AT = (3, 2), (6, 1), (13, 3), (14, 1)

        def piece(b, k):
            return 4 * b + (k - 1)

        def score_bank(i):
            return SB[1 if i == 15 else i % 3]

        def turned_bank(b, c, k):
            return (ST + SB)[k % 4 if is_last(b, c) else k % 2]

        def is_last(b, c):
            return isinstance(b, int) and (b, c) == (B - 1, NG - 1)

        def hold(eng, s, value):
            if isinstance(value, int):
                if value > 0:
                    eng.wait_ge(s, value)
            else:
                eng.wait_ge(s, value)

        def hold_apart(eng, s, value):
            hold(eng, s, value)
            if not isinstance(value, int):
                eng.sem_inc(passed, 1)

        block = ctx.enter_context(nc.Block())
        NFIRST, NREST, NLATE = 5, 12, 10
        LOADS = 8

        @block.sync
        def _(sp):
            def take(s, dst, src):
                sp.dma_start(dst, src).then_inc(s, 16)

            sp.sem_inc(out_done, 16)
            take(in_first, wqk_sb[:, :, :], wqk)
            take(in_first, hsT_sb[:, 0:S], hsT[:, 0:S])
            take(in_first, bqk_sb[:, :], bqk)
            take(in_first, fac_sb[0][:, :, :], fac_q)
            take(in_first, fac_sb[1][:, :, :], fac_k)
            take(in_rest, wap_sb[:, :], wap)
            take(in_rest, hsT_sb[:, S:B * S], hsT[:, S:B * S])
            take(in_rest, wvn_sb[:, :], wv_nat)
            take(in_rest, mix_sb[:, :], mixbd)
            take(in_rest, wv_sb[:, 0:D], wv)
            take(in_rest, bvc_sb[:, :], bv_col)
            take(in_rest, bap_sb[:, :], bap.partition_broadcast(P))
            take(in_rest, bvv_sb[:, 0:D], bv_row.partition_broadcast(P))
            take(in_rest, bvv_sb[:, D:2 * D], mixb.partition_broadcast(P))
            take(in_rest, km_sb[:, :], kmask)
            take(in_rest, fix_sb[:, :], diagfix)
            take(in_rest, id_sb[:, :], ident)

            def take_late():
                take(in_late, kern_sb[:, :], kern)
                take(in_late, sc_sb[:, 0:1], s_in.partition_broadcast(P))
                take(in_late, sc_sb[:, 1:2], s_k.partition_broadcast(P))
                for h_ in range(2):
                    take(in_late, hs_sb[:, h_ * 8:h_ * 8 + 8, :], hs.rearrange("(i p) d -> p i d", p=P)[:, h_ * 8:h_ * 8 + 8, :])
                take(in_late, wo_sb[:, :], wo)
                take(in_late, bo_sb[:, :], bo.partition_broadcast(P))
                take(in_late, g_sb[:, :], ln_g.partition_broadcast(P))
                take(in_late, b_sb[:, :], ln_b.partition_broadcast(P))
                take(in_late, fb_sb[:, :], fbias.partition_broadcast(P))

            def store(what, b, k, s):
                sp.dma_start(scratch[b, k % 2, k // 2].rearrange("f p r h n -> (r h) (f p) n"),
                             what.rearrange("p f a n -> p (f a) n")).then_inc(s, 16)

            def store_parts(b, k):
                hold_apart(sp, parts_ready, piece(b, k))
                store(parts[:, :, :, :], b, k, parts_stored)

            def load_stacks(b, c):
                bb, g = (b, c) if c < NG else (b + 1, c - NG)
                hold_apart(sp, st_ready, 64 * b + 16 * (c - 3))
                if isinstance(bb, int) and bb == 0 and g < 2:
                    sp.wait_ge(early_stored, 32)
                else:
                    hold_apart(sp, parts_stored, 64 * bb + 32 * (g // 2))
                for row, n in GROUPS:
                    part = 3 - n
                    stack = lambda st_: st_[row:row + n * R, g, :, :, :].rearrange("p f j n -> p f (j n)")
                    from_ = lambda side, p0, p1: scratch[bb, side, g // 2, :, p0:p1, :, 4 * (g % 2):4 * (g % 2) + 4, :]\
                        .rearrange("f p r h n -> (p r) f (h n)")
                    sp.dma_start(stack(Kst), from_(1, 0, n)).then_inc(stacks_in[g], 16)
                    for f in range(2) if n > 1 else ():
                        one = scratch[bb, 0, g // 2, f, part, :, 4 * (g % 2):4 * (g % 2) + 4, :]\
                            .rearrange("r h n -> r (h n)").unsqueeze(0).broadcast_to([n, R, GH * S])
                        sp.dma_start(Qst[row:row + n * R, g, f, :, :].rearrange("p j n -> p (j n)"), one)\
                            .then_inc(stacks_in[g], 16)
                    if n == 1:
                        sp.dma_start(stack(Qst), from_(0, part, part + 1)).then_inc(stacks_in[g], 16)

            for k in range(2):
                sp.wait_ge(early_split, 5 * k + 5)
                store(parts_early[k], 0, k, early_stored)
            load_stacks(0, 0)
            store_parts(0, 2)
            load_stacks(0, 1)
            store_parts(0, 3)
            sp.wait_ge(const_set, 5)
            for g in range(1, NG):
                if g == NG - 1:
                    sp.wait_ge(v_mixed, 5)
                sp.dma_start(Kst[KR:KR + MP, g, :, :, :].rearrange("p f j n -> p (f j n)"),
                             Kst[KR:KR + MP, 0, :, :, :].rearrange("p f j n -> p (f j n)")).then_inc(ones_set, 16)
                if g == 1:
                    load_stacks(0, 2)
                    take_late()

            def write_out(b):
                hold_apart(sp, c_dve, DVE_C * b + DVE_C)
                sp.dma_start(out[b].rearrange("(t p) d -> p t d", p=P), x1[:, :, :]).then_inc(out_done, 16)

            def body(b, first=False, last=False):
                for c in range(NG):
                    if not last:
                        store_parts(b + 1, c)
                    if not last or c == 0:
                        load_stacks(b, c + 3)
                if not first:
                    write_out(b - 1)

            body(0, first=True)
            with sp.Fori(1, B - 1) as b:
                body(b)
            body(B - 1, last=True)
            write_out(B - 1)
            sp.wait_ge(out_done, 16 * B + 16)

        @block.tensor
        def _(pe):
            mm = nc.tensor.matmul

            def project(b, k, wait_sem, wait_value, bank=MB, done=proj_ready):
                hold(pe, wait_sem, wait_value)
                mm(bank[:, :], wqk_sb[:, k, :], hsT_sb[:, bass.ds(b * S, S)] if not isinstance(b, int)
                   else hsT_sb[:, b * S:b * S + S], start=True, stop=True).then_inc(done, 1)

            def entangled(b, c, j):
                g = c % NG
                if j == 0:
                    hold(pe, stacks_in[g], (LOADS * 16) * b + (LOADS * 16) * (1 + c // NG))
                hold(pe, ek_alone_ready, 16 * b + (4 * c + j + 1))
                hold(pe, fixed_ready, 16 * b + (4 * c + j))
                for t in range(NT):
                    tile = slice(t * P, t * P + P)
                    e = mm(EB[:, tile], Qst[0:KR, g, 0, j, tile], Kd[0:KR, j % 2, 1, tile], start=True, stop=True)
                e.then_inc(e_ready, 1)

            def scores(b, c, j, t):
                g = c % NG
                tile = slice(t * P, t * P + P)
                i = 4 * j + t
                hold(pe, r_ready, 64 * b + (16 * c + i - (1 if i in (1, 15) else 2)))
                bank = score_bank(i)
                if t == 0:
                    hold(pe, k_alone_ready, 16 * b + (4 * c + j + 1))
                s = mm(bank[:, tile], Qst[0:KR, g, 0, j, tile], Kd[0:KR, j % 2, 0, tile], start=True, stop=True)
                if t > 0:
                    s = mm(bank[:, 0:t * P], Qst[0:KR, g, 0, j, tile], Kst[0:KR, g, 0, j, 0:t * P],
                           start=True, stop=True)
                if t < NT - 1:
                    s = mm(bank[:, (t + 1) * P:S], Qst[0:KR, g, 1, j, tile],
                           Kst[0:KR, g, 1, j, (t + 1) * P:S], start=True, stop=True)
                s.then_inc(s_ready, 1)

            KM = KR + MP

            def scores_t(b, c, t, j):
                g = c % NG
                if t == 0 and j == 0:
                    hold(pe, mrows_in, 128 * b + 32 * (c + 1))
                    if isinstance(b, int) and b == c == 0:
                        pe.wait_ge(ones_set, 16 * (NG - 1))
                        pe.wait_ge(const_set, 5)
                    hold(pe, rm_ready, 16 * b + 4 * (c + 1))
                tile = slice(t * P, t * P + P)
                k = 4 * t + j
                if is_last(b, c) and k in (2, 3):
                    pe.wait_ge(r_ready, 16 * NG * B)
                else:
                    hold(pe, exp_ready, 64 * b + (16 * c + k - (3 if is_last(b, c) and k > 3 else 1)))
                bank = turned_bank(b, c, k)
                s = mm(bank[:, tile], Rm[:, c % 2, j, t, :], id_sb[:, :], start=True, stop=True, is_transpose=True)
                if t < NT - 1:
                    s = mm(bank[:, (t + 1) * P:S], Kst[0:KM, g, 0, j, tile], Qst[0:KM, g, 0, j, (t + 1) * P:S],
                           start=True, stop=True)
                if t > 0:
                    s = mm(bank[:, 0:t * P], Kst[0:KM, g, 1, j, tile], Qst[0:KM, g, 1, j, 0:t * P],
                           start=True, stop=True)
                s.then_inc(st_ready, 1)

            def contexts(b, c, t):
                if t == 0:
                    hold(pe, v_ready, 4 * b + (c + 1))
                    hold(pe, ct_copied, 4 * b + c)
                hold(pe, exp_ready, 64 * b + (16 * c + 4 * t + 4))
                for j in range(GH):
                    m = mm(CB[32 * j:32 * j + 32, :], Vst[:, c % 2, t, j, :], PT[:, t % 2, j, :],
                           start=(t == 0), stop=(t == NT - 1))
                m.then_inc(pv_ready, 1)

            def maxima_t(b, c, first):
                hold(pe, msplit, 16 * b + 4 * (c + 1))
                if first and c == 0:
                    hold(pe, early_split, 1)
                if not (first and c < 2):
                    hold(pe, ctx_normed, 8 * b + (2 * c - 2))
                if not first and c == 1:
                    hold(pe, c_act, ACT_C * (b - 1) + 1)
                mm(MBh[:, 0:P], mparts[:, :], idb_sb[:, :],
                   start=True, stop=True, is_transpose=True).then_inc(mt_ready, 1)

            def turn_contexts(b, c, last_product):
                hold(pe, ct_copied, 4 * b + (c + 1))
                hold(pe, c_dve, last_product)
                hold(pe, ctx_normed, 8 * b + 2 * c)
                for t in range(NT):
                    m = mm(MB[:, t * P:t * P + P], CT[:, c % 2, t * P:t * P + P], id_sb[:, :],
                           start=True, stop=True, is_transpose=True)
                m.then_inc(ctx_turned, 1)

            def ending(b, slot, i):
                n = lambda x: PE_C * b + x
                after_dve = lambda x: hold(pe, c_dve, DVE_C * b + x)
                if (slot, i) == NORMED_AT:
                    hold(pe, ctx_normed, 8 * b + 8)
                    for t in range(NT):
                        m = mm(MB[:, t * P:t * P + P], cn[:, t, :], id_sb[:, :], start=True, stop=True, is_transpose=True)
                    m.then_inc(c_pe, 1)
                if (slot, i) == OUTPUT_AT:
                    hold(pe, c_act, ACT_C * b + 1)
                    for t in range(NT):
                        m = mm(MB[:, t * P:t * P + P], cnT[:, t * P:t * P + P], wo_sb[:, :], start=True, stop=True)
                    m.then_inc(c_pe, 1)
                if (slot, i) == QUANTIZED_AT:
                    after_dve(33)
                    for t in range(NT):
                        m = mm(MBh[:, t * P:t * P + P], xq[:, t, :], idb_sb[:, :], start=True, stop=True, is_transpose=True)
                    m.then_inc(c_pe, 1)
                if (slot, i) == FFN_AT:
                    hold(pe, c_act, ACT_C * b + 4)
                    for t in range(NT):
                        m = mm(MB[:, t * P:t * P + P], xqT[:, t * P:t * P + P], kq_sb[:, :], start=True, stop=True)
                    m.then_inc(c_pe, 1)

            pe.wait_ge(in_first, 16 * NFIRST)
            for k in range(4):
                project(0, k, None, 0, (MB, EB, SB[0], SB[1])[k], early_ready if k < 2 else proj_ready)
            pe.wait_ge(in_rest, 16 * NREST)
            mm(ST[0][:, 0:D], wvn_sb[:, :], mix_sb[:, :], start=True, stop=True)
            pe.wait_ge(vprep, 1)
            mm(ST[0][:, D:2 * D], bvb_sb[:, :], mix_sb[:, :], start=True, stop=True).then_inc(vp_ready, 1)
            for i in range(B * NT):
                m = mm(ST[1][:, i * 2 * H:(i + 1) * 2 * H], hsT_sb[:, i * P:i * P + P], wap_sb[:, :],
                       start=True, stop=True)
            m.then_inc(vp_ready, 1)
            pe.wait_ge(vprep, 3)

            def value_products(i):
                hold(pe, vp_copied, i - 1)
                for h_ in range(2):
                    m = mm(VP[i % 2][:, h_ * 2 * D:(h_ + 1) * 2 * D],
                           hsT_sb[:, (2 * i + h_) * P:(2 * i + h_ + 1) * P], wv_sb[:, :], start=True, stop=True)
                m.then_inc(vp_ready, 1)

            pe.wait_ge(early_split, 6)
            entangled(0, 0, 0)
            pe.wait_ge(proj_copied, 2)
            for j in range(GH):
                for t in range(NT):
                    scores(0, 0, j, t)
                    if j == 0 and t == 1:
                        pe.wait_ge(vprep, 4)
                    if t % 2 == 1:
                        value_products(2 * j + t // 2)
                    if t == 3:
                        entangled(0, (j + 1) // GH, (j + 1) % GH)
            pe.wait_ge(vp_copied, B * NT // 2)
            def step(b, c, t, first, last):
                for i in range(NT):
                    if not (last and c == NG - 1):
                        scores(b, c + 1, t, i)
                    n_ = 4 * (c + 1) + t + 1
                    if i == 3 and not (last and n_ >= H):
                        entangled(b, n_ // 4, n_ % 4)
                    k = 4 * t + i - LAG
                    if not (first and c == 0 and k < 0):
                        scores_t(b, c - (k < 0), k % 16 // 4, k % 4)
                    if i == 2 and not (first and c == 0 and t < 3):
                        contexts(b, c - (t < 3), (t - 3) % NT)
                    if (t, i) == ((0, 0) if last and c == NG - 1 else MAXIMA_AT):
                        maxima_t(b, c, first)
                    if (t, i) == (1, 0) and not last:
                        project(b + 1, c, mt_copied, 4 * b + (c + 1))
                    if (t, i) == (1, 3) and not last:
                        hold(pe, proj_copied, piece(b + 1, c))
                    if (t, i) == (3, 1) and not (first and c == 0):
                        if c == 3 and not first:
                            hold(pe, c_act, ACT_C * (b - 1) + 5)
                        turn_contexts(b, c - 1, DVE_C * (b - 1) + 1 if c == 1 and not first else 0)
                    if not first:
                        ending(b - 1, 4 * c + t, i)

            def body(b, first=False, last=False):
                for c in range(NG):
                    for t in range(NT):
                        step(b, c, t, first, last)

            body(0, first=True)
            with pe.Fori(1, B - 1) as b:
                body(b)
            body(B - 1, last=True)
            for k in range(16 - LAG, 16):
                if k == 12:
                    contexts(B - 1, NG - 1, 1)
                scores_t(B - 1, NG - 1, k // 4, k % 4)
            contexts(B - 1, NG - 1, 2)
            contexts(B - 1, NG - 1, 3)
            turn_contexts(B - 1, NG - 1, 0)
            for slot in range(16):
                for i in range(4):
                    ending(B - 1, slot, i)

        @block.scalar
        def _(act):
            def copy_proj(b, k, bank=MB):
                hold(act, proj_ready, piece(b, k))
                hold(act, faced_ready, piece(b, k) - 1)
                nc.scalar.activation(proj[:, :], bank[:, :], ACT.Identity, bias=bqk_sb[:, k:k + 1])\
                    .then_inc(proj_copied, 1)

            def cast_hi(b, k):
                hold(act, faced_ready, piece(b, k))
                hold(act, parts_stored, 64 * b + 16 * (k - 2))
                nc.scalar.activation(parts[:, :, 0, :], faced[:, :, :], ACT.Copy).then_inc(hi_ready, 1)

            def cast_mid(b, k):
                hold(act, left_ready, piece(b, k))
                nc.scalar.activation(parts[:, :, 1, :], faced[:, :, :], ACT.Copy).then_inc(mid_ready, 1)

            def place_maxima(b, c):
                hold(act, mt_copied, 4 * b + (c + 1))
                for f in range(2):
                    act.dma_start(Qst[KR:KR + MP, c, f, :, :].rearrange("p j n -> p (j n)"), mrows[:, :])\
                        .then_inc(mrows_in, 16)

            def k_alone(b, c, j):
                g = c % NG
                if j == 0:
                    hold(act, stacks_in[g], (LOADS * 16) * b + (LOADS * 16) * (1 + c // NG))
                hold(act, s_ready, 64 * b + (16 * c + 4 * j - 4))
                nc.scalar.activation(Kd[0:KR, j % 2, 0, :], Kst[0:KR, g, 0, j, :], ACT.Copy, scale=km_sb[0:KR, 0:1])\
                    .then_inc(k_alone_ready, 1)

            def exps(b, c, t, j):
                if j == 0:
                    hold(act, pv_ready, 16 * b + (4 * c + t - 1))
                hold(act, st_ready, 64 * b + (16 * c + 4 * t + j + 1))
                nc.scalar.activation(PT[:, t % 2, j, :], turned_bank(b, c, 4 * t + j)[:, :], ACT.Exp).then_inc(exp_ready, 1)

            def copy_contexts(b, c):
                hold(act, pv_ready, 16 * b + 4 * (c + 1))
                hold(act, ctx_turned, 4 * b + (c - 1))
                nc.scalar.activation(CT[:, c % 2, :], CB[:, :], ACT.Copy).then_inc(ct_copied, 1)

            def ending(b, slot, j):
                if (slot, j) == (4, 0):
                    hold(act, c_pe, PE_C * b + 1)
                    nc.scalar.activation(cnT[:, :], MB[:, :], ACT.Copy).then_inc(c_act, 1)
                if (slot, j) == (11, 3):
                    hold(act, c_dve, DVE_C * b + 25)
                    nc.scalar.activation(xb[:, :, :], x2[:, :, :], ACT.Copy).then_inc(c_act, 1)
                if (slot, j) == (12, 0):
                    hold(act, c_act, ACT_C * b + 2)
                    nc.scalar.activation(q1[:, :, :], xb[:, :, :], ACT.Copy, scale=rs_sb[:, 0:1]).then_inc(c_act, 1)
                if (slot, j) == (14, 0):
                    hold(act, c_pe, PE_C * b + 3)
                    nc.scalar.activation(xqT[:, :], MBh[:, 0:S], ACT.Copy).then_inc(c_act, 1)
                if (slot, j) == (14, 3):
                    hold(act, c_pe, PE_C * b + PE_C)
                    hold_apart(act, c_act, ACT_C * b + 4)
                    product = MB[:, :].rearrange("p (t n) -> p t n", t=NT)
                    nc.scalar.activation(xb[:, :, :], product, ACT.Copy, scale=ss_sb[:, 0:1]).then_inc(c_act, 1)

            act.wait_ge(in_first, 16 * NFIRST)
            copy_proj(0, 2, SB[0])
            cast_hi(0, 2)
            copy_proj(0, 3, SB[1])
            cast_mid(0, 2)
            act.wait_ge(in_rest, 16 * NREST)
            act.wait_ge(vprep, 4)
            co = lambda i: co_sb[:, i, :].rearrange("p (i h) -> p i h", h=H)
            nc.scalar.activation(co(0), ap_sb[:, :, 0:H], ACT.Exp, scale=-1.0).then_inc(vact, 1)
            nc.scalar.activation(co(1), ap_sb[:, :, H:2 * H], ACT.Tanh).then_inc(vact, 1)
            act.wait_ge(vact, 2)
            nc.scalar.activation(co_sb[:, 2, :], co_sb[:, 1, :], ACT.Sin, scale=math.pi).then_inc(vact, 1)
            act.wait_ge(const_set, 2)
            act.wait_ge(vprep, 5)
            nc.scalar.activation(co_sb[:, 3, :], co_sb[:, 3, :], ACT.Sin, scale=-math.pi, bias=halfpi[:, :])\
                .then_inc(vact, 1)
            k_alone(0, 0, 0)
            k_alone(0, 0, 1)
            cast_hi(0, 3)
            cast_mid(0, 3)
            for n_ in range(2, GH + 1):
                k_alone(0, n_ // GH, n_ % GH)

            def body(b, first=False, last=False):
                for c in range(NG):
                    for t in range(NT):
                        for j in range(GH):
                            if not first:
                                ending(b - 1, 4 * c + t, j)
                            k = 4 * t + j - LAG
                            if not (first and c == 0 and k < 0):
                                exps(b, c - (k < 0), k % 16 // 4, k % 4)
                            n_ = 4 * (c + 1) + t + 1
                            if j == 1 and not (last and n_ >= H):
                                k_alone(b, n_ // 4, n_ % 4)
                            if (t, j) == (2, 3) and not (first and c == 0):
                                copy_contexts(b, c - 1)
                            if (t, j) == ((0, 1) if last and c == NG - 1 else (0, 2)):
                                place_maxima(b, c)
                            if not last and (t, j) == (1, 0):
                                copy_proj(b + 1, c)
                            if not last and (t, j) == (2, 0):
                                cast_hi(b + 1, c)
                            if not last and (t, j) == (3, 0):
                                cast_mid(b + 1, c)

            body(0, first=True)
            with act.Fori(1, B - 1) as b:
                body(b)
            body(B - 1, last=True)
            for k in range(16 - LAG, 16):
                exps(B - 1, NG - 1, k // 4, k % 4)
            copy_contexts(B - 1, NG - 1)
            for slot in range(16):
                for j in range(4):
                    ending(B - 1, slot, j)

        @block.gpsimd
        def _(pool):
            pool.memset(neghalf[:, :], -0.5).then_inc(const_set, 1)
            pool.memset(halfpi[:, :], math.pi / 2).then_inc(const_set, 1)
            pool.memset(Vst[:, :, :, :, :], 0.0).then_inc(const_set, 1)
            pool.wait_ge(const_set, 3)
            pool.memset(Vst[:, :, :, :, HD:HD + 1], 1.0).then_inc(const_set, 1)
            pool.wait_ge(const_set, 4)
            pool.memset(Kst[KR:KR + MP, 0, :, :, :], 1.0).then_inc(const_set, 1)
            pool.wait_ge(in_first, 16 * NFIRST)
            pool.wait_ge(const_set, 5)

            def split(b, k, step):
              if step == 0:
                hold(pool, proj_copied, piece(b, k))
                hold(pool, parts_ready, piece(b, k) - 1)
                both = proj[:, :].unsqueeze(1).broadcast_to([P, 2, S])
                nc.gpsimd.tensor_tensor(faced[:, :, :], both, fac_sb[k % 2][:, :, :], ALU.mult)\
                    .then_inc(faced_ready, 1)
              if step == 1:
                hold(pool, hi_ready, piece(b, k))
                nc.gpsimd.tensor_tensor(faced[:, :, :], faced[:, :, :], parts[:, :, 0, :], ALU.subtract)\
                    .then_inc(left_ready, 1)
              if step == 2:
                hold(pool, mid_ready, piece(b, k))
                nc.gpsimd.tensor_tensor(parts[:, :, 2, :], faced[:, :, :], parts[:, :, 1, :], ALU.subtract)\
                    .then_inc(parts_ready, 1)

            def less_maxima(b, c, j):
                g = c % NG
                hold(pool, r_ready, 16 * (4 * b) + (16 * c + 4 * j + 4))
                hold(pool, st_ready, 16 * (4 * b) + 16 * (c - 1))
                m = mx[:, g % 2, NT * j:NT * j + NT].unsqueeze(2).broadcast_to([P, NT, P])
                nc.gpsimd.tensor_tensor(Rm[:, g % 2, j, :, :], scored_diag[j % 2], m, ALU.subtract).then_inc(rm_ready, 1)

            def place_values(b, c):
                hold_apart(pool, pv_ready, 16 * b + 4 * (c - 1))
                if isinstance(b, int):
                    src = V[:, b * NT:b * NT + NT, c * GH:c * GH + GH, :]
                else:
                    src = V[:, bass.ds(b * NT, NT), c * GH:c * GH + GH, :]
                pool.tensor_copy(Vst[:, c % 2, :, :, 0:HD], src).then_inc(v_ready, 1)

            def ending(b, slot):
                def reciprocal_root(before, n):
                    hold_apart(pool, c_dve, DVE_C * b + before)
                    pool.tensor_scalar(ve[:, :], mv[:, :, 1], EPS, None, ALU.add).then_inc(c_pool, 1)
                    hold(pool, c_pool, POOL_C * b + n)
                    nc.gpsimd.tensor_tensor(rstd[:, :], ve[:, :], neghalf[:, :], ALU.pow).then_inc(c_pool, 1)

                rows = lambda x: x[:, :].unsqueeze(1).broadcast_to([P, NT, D])
                h_ = hs_sb[:, b * NT:b * NT + NT, :] if isinstance(b, int) else hs_sb[:, bass.ds(b * NT, NT), :]
                if slot == 1:
                    if isinstance(b, int):
                        pool.wait_ge(in_late, 16 * NLATE)
                    nc.gpsimd.tensor_tensor(hs_bo[:, :, :], h_, rows(bo_sb), ALU.add).then_inc(c_pool, 1)
                if slot == 2:
                    nc.gpsimd.tensor_tensor(hs_b[:, :, :], h_, rows(b_sb), ALU.add).then_inc(c_pool, 1)
                if slot == 8:
                    reciprocal_root(9, 3)
                if slot == 9:
                    hold(pool, c_dve, DVE_C * b + 13)
                    nc.gpsimd.tensor_tensor(x1[:, :, :], x1[:, :, :], rows(g_sb), ALU.mult).then_inc(c_pool, 1)
                    hold_apart(pool, c_pool, POOL_C * b + 5)
                    nc.gpsimd.tensor_tensor(x1[:, :, :], x1[:, :, :], hs_b[:, :, :], ALU.add).then_inc(c_pool, 1)
                if slot == 11:
                    reciprocal_root(21, 7)
                if slot == 15:
                    reciprocal_root(43, 9)

            for k in (2, 3):
                for step in range(3):
                    split(0, k, step)
            def mix(part, stage):
                tiles = slice(0, HALF) if part == 0 else slice(HALF + 2 * part - 2, HALF + 2 * part)
                sup = VS[part][:, :, D:2 * D].rearrange("p i (h d) -> p i h d", d=HD)
                val = VS[part][:, :, 0:D].rearrange("p i (h d) -> p i h d", d=HD)
                dst = V[:, tiles, :, :]
                fac = lambda i, n: factor[i].rearrange("p (i h) -> p i h", h=H)[:, tiles, :].unsqueeze(3)\
                    .broadcast_to([P, tiles.stop - tiles.start, H, n])
                tt = nc.gpsimd.tensor_tensor
                if stage == 0:
                    if part:
                        pool.wait_ge(v_mixed, 5 * part)
                    tt(dst, sup, fac(3, HD), ALU.mult).then_inc(v_mixed, 1)
                    pool.wait_ge(v_mixed, 5 * part + 1)
                    tt(val, val, dst, ALU.add).then_inc(v_mixed, 1)
                if stage == 1:
                    pool.wait_ge(v_mixed, 5 * part + 2)
                    tt(dst[:, :, :, 1:HD], sup[:, :, :, 0:HD - 1], fac(2, HD - 1), ALU.mult).then_inc(v_mixed, 1)
                    tt(dst[:, :, :, 0:1], sup[:, :, :, HD - 1:HD], fac(2, 1), ALU.mult).then_inc(v_mixed, 1)
                    pool.wait_ge(v_mixed, 5 * part + 4)
                    tt(dst, val, dst, ALU.add).then_inc(v_mixed, 1)

            less_maxima(0, 0, 0)
            less_maxima(0, 0, 1)
            pool.wait_ge(vprep, 10)
            pool.wait_ge(vp_copied, B * NT // 4)
            mix(0, 0)
            less_maxima(0, 0, 2)
            mix(0, 1)
            less_maxima(0, 0, 3)
            pool.wait_ge(v_mixed, 5)

            def body(b, first=False, last=False):
                for c in range(NG):
                    for j in range(GH):
                        if not first:
                            ending(b - 1, 4 * c + j)
                        if j == 0:
                            place_values(b, c)
                            if not last:
                                split(b + 1, c, 0)
                        if not (last and c == NG - 1):
                            less_maxima(b, c + 1, j)
                        if first and (c, j) in ((0, 3), (1, 3), (2, 1), (3, 3)):
                            if c == 0:
                                pool.wait_ge(vp_copied, B * NT // 2)
                            for stage in range(2):
                                mix(c + 1, stage)
                        if first and (c, j) == (3, 3):
                            pool.wait_ge(v_mixed, 25)
                        if not last and (j == 1 or j == 2 + (c == 2)):
                            split(b + 1, c, min(j, 2))

            body(0, first=True)
            with pool.Fori(1, B - 1) as b:
                body(b)
            body(B - 1, last=True)
            for slot in range(16):
                ending(B - 1, slot)

        @block.vector
        def _(dve):
            v = nc.vector
            bc = lambda x, n=NT: x[:, :].unsqueeze(1).broadcast_to([P, n, D])
            v.memset(fixed_all[:, :], 0.0).then_inc(k_dve, 1)
            v.memset(mparts[:, :], 0.0).then_inc(k_dve, 1)
            dve.wait_ge(in_first, 16 * NFIRST)
            n_early = [0]

            def early(ins):
                n_early[0] += 1
                ins.then_inc(early_split, 1)
                dve.wait_ge(early_split, n_early[0])

            for k, bank in ((0, MB), (1, EB)):
                dve.wait_ge(early_ready, k + 1)
                early(v.scalar_tensor_tensor(out=faced_early, in0=bank[:, :].unsqueeze(1).broadcast_to([P, 2, S]),
                                             scalar=bqk_sb[:, k:k + 1], in1=fac_sb[k][:, :, :],
                                             op0=ALU.add, op1=ALU.mult))
                part = lambda i: parts_early[k][:, :, i, :]
                early(v.tensor_copy(part(0), faced_early))
                early(v.tensor_tensor(faced_early, faced_early, part(0), ALU.subtract))
                early(v.tensor_copy(part(1), faced_early))
                early(v.tensor_tensor(part(2), faced_early, part(1), ALU.subtract))
            dve.wait_ge(in_rest, 16 * NREST)
            v.tensor_copy(bvb_sb[:, :], bvc_sb[:, 0:1].broadcast_to([P, P])).then_inc(vprep, 1)
            dve.wait_ge(vp_ready, 1)
            v.tensor_copy(wv_sb[:, D:2 * D], ST[0][:, 0:D]).then_inc(vprep, 1)
            v.tensor_tensor(bvv_sb[:, D:2 * D], bvv_sb[:, D:2 * D], ST[0][:, D:2 * D], ALU.add).then_inc(vprep, 1)
            dve.wait_ge(vp_ready, 2)
            v.tensor_tensor(ap_sb[:, :, :], ST[1][:, :].rearrange("p (i n) -> p i n", n=2 * H),
                            bap_sb[:, :].unsqueeze(1).broadcast_to([P, B * NT, 2 * H]), ALU.add).then_inc(vprep, 1)
            dve.wait_ge(vprep, 4)

            def place_products(i):
                dve.wait_ge(vp_ready, 3 + i)
                dst = VS[0][:, 2 * i:2 * i + 2, :] if 2 * i < HALF else VS[1 + i - HALF // 2][:, :, :]
                v.tensor_tensor(dst,
                                VP[i % 2][:, :].rearrange("p (i n) -> p i n", i=2),
                                bvv_sb[:, :].unsqueeze(1).broadcast_to([P, 2, 2 * D]), ALU.add).then_inc(vp_copied, 1)

            dve.wait_ge(vact, 2)
            chain = [5]

            def link(ins):
                chain[0] += 1
                ins.then_inc(vprep, 1)
                dve.wait_ge(vprep, chain[0])

            v.tensor_scalar(co_sb[:, 3, :].bitcast(u32), co_sb[:, 1, :].bitcast(u32), 0x7FFFFFFF, None, ALU.bitwise_and).then_inc(vprep, 1)
            dve.wait_ge(vprep, 5)
            link(v.tensor_scalar(co_sb[:, 0, :], co_sb[:, 0, :], 1.0, None, ALU.add))
            link(v.reciprocal(co_sb[:, 0, :], co_sb[:, 0, :]))
            link(v.tensor_scalar(co_sb[:, 0, :], co_sb[:, 0, :], SUP, None, ALU.mult))

            def value_factors():
                dve.wait_ge(vact, 4)
                v.tensor_tensor(factor[3], co_sb[:, 3, :], co_sb[:, 0, :], ALU.mult).then_inc(vprep, 1)
                v.tensor_tensor(factor[2], co_sb[:, 2, :], co_sb[:, 0, :], ALU.mult).then_inc(vprep, 1)

            kk = [2]

            def klink(ins, chained=True):
                kk[0] += 1
                ins.then_inc(k_dve, 1)
                if chained:
                    dve.wait_ge(k_dve, kk[0])

            klink(v.tensor_copy(idb_sb[:, :], id_sb[:, :]))
            def quantize(dst, src, a, t1, t2, scale, step, part=(0, 9), n=None, base=0, settle=None):
                if n is not None:
                    n[0] = base + part[0]
                    settle()
                bits = lambda x: x.bitcast(u32)
                for k in range(*part):
                    if k == 0:
                        ins = v.tensor_scalar(a, src, scale, None, ALU.mult)
                    if k == 1:
                        ins = v.tensor_scalar(bits(t1), bits(a), 0x7F800000, None, ALU.bitwise_and)
                    if k == 2:
                        ins = v.tensor_scalar(t1, t1, 2.0 ** -6, 1.5 * 2.0 ** 20, ALU.max, ALU.mult)
                    if k == 3:
                        ins = v.tensor_tensor(a, a, t1, ALU.add)
                    if k == 4:
                        ins = v.tensor_tensor(a, a, t1, ALU.subtract)
                    if k == 5:
                        ins = v.tensor_tensor(t1, a, a, ALU.mult)
                    if k == 6:
                        ins = v.tensor_scalar(t1, t1, 448.0 ** 2, 3e38, ALU.is_gt, ALU.mult)
                    if k == 7:
                        ins = v.tensor_scalar(t1, t1, 3e38, 0.0, ALU.mult, ALU.mult)
                    if k == 8:
                        ins = v.tensor_tensor(dst, a, t1, ALU.add)
                    step(ins, n is None or k < part[1] - 1)

            QUANTIZE_AT = {(12, 1): (1, 2), (12, 2): (2, 4), (12, 3): (4, 5), (13, 0): (5, 6),
                           (13, 1): (6, 8), (13, 2): (8, 9)}

            def quantize_kernel(k):
                if k == 0:
                    dve.wait_ge(in_late, 16 * NLATE)
                    klink(v.reciprocal(rs_sb[:, :], sc_sb[:, :]), False)
                if k == 1:
                    dve.wait_ge(k_dve, kk[0])
                    klink(v.tensor_tensor(ss_sb[:, :], sc_sb[:, 0:1], sc_sb[:, 1:2], ALU.mult), False)
                if 2 <= k < 11:
                    quantize(kq_sb[:, :], kern_sb[:, :], q1[:, 0, :], q2[:, 0, :], None, rs_sb[:, 1:2], klink,
                             (k - 2, k - 1), [0], 0, lambda: dve.wait_ge(k_dve, kk[0]))

            def k_stacks(b, c, j):
                g = c % NG
                if j == 0:
                    hold(dve, stacks_in[g], (LOADS * 16) * b + (LOADS * 16) * (1 + c // NG))
                hold(dve, s_ready, 64 * b + (16 * c + 4 * j - 4))
                v.tensor_scalar(Kd[0:KR, j % 2, 1, :], Kst[0:KR, g, 0, j, :], km_sb[0:KR, 1:2], None, ALU.mult)\
                    .then_inc(ek_alone_ready, 1)

            def fix_diagonal(b, c, j):
                hold(dve, e_ready, 16 * b + (4 * c + j + 1))
                hold(dve, r_ready, 64 * b + (16 * c + 4 * j))
                v.tensor_tensor(fixed_diag, EB[:, :].rearrange("p (t n) -> p t n", t=NT), bc(fix_sb), ALU.mult)\
                    .then_inc(fixed_ready, 1)

            def complete(b, c, j, t):
                g = c % NG
                hold_apart(dve, s_ready, 64 * b + (16 * c + 4 * j + t + 1))
                if t == 0:
                    hold_apart(dve, fixed_ready, 16 * b + (4 * c + j + 1))
                    hold_apart(dve, rm_ready, 16 * b + (4 * c + j - 1))
                v.tensor_tensor_reduce(out=scored[j % 2][:, t, :], in0=score_bank(4 * j + t)[:, :], in1=fixed[:, t, :], scale=1.0,
                                       scalar=NEG, op0=ALU.add, op1=ALU.max,
                                       accum_out=mx[:, g % 2, NT * j + t:NT * j + t + 1]).then_inc(r_ready, 1)

            def split_maxima(b, c):
                g = c % NG
                m = mx[:, g % 2, :]
                x = lambda k: 16 * b + (4 * c + k)
                hold(dve, r_ready, 64 * b + (16 * c + 16))
                hold(dve, mt_ready, 4 * b + c)
                v.tensor_scalar(mpart(0), m, -1.0, None, ALU.mult).then_inc(msplit, 1)
                hold(dve, msplit, x(1))
                v.scalar_tensor_tensor(out=mneg[:, :], in0=m, scalar=-1.0, in1=mpart(0),
                                       op0=ALU.mult, op1=ALU.subtract).then_inc(msplit, 1)
                hold(dve, msplit, x(2))
                v.tensor_copy(mpart(1), mneg[:, :]).then_inc(msplit, 1)
                hold(dve, msplit, x(3))
                v.tensor_tensor(mpart(2), mneg[:, :], mpart(1), ALU.subtract).then_inc(msplit, 1)

            def copy_maxima(b, c):
                hold(dve, mt_ready, 4 * b + (c + 1))
                hold(dve, mrows_in, 128 * b + 32 * c)
                v.tensor_copy(mrows[:, :], MBh[0:MP * GH * NT, 0:P]).then_inc(mt_copied, 1)

            def norm_contexts(b, c):
                hold(dve, ctx_turned, 4 * b + (c + 1))
                whole = MB[:, :].rearrange("p (t h n) -> p t h n", t=NT, n=32)
                v.reciprocal(rden[:, :, :], whole[:, :, :, HD]).then_inc(ctx_normed, 1)
                hold(dve, ctx_normed, 8 * b + (2 * c + 1))
                g = c % NG
                v.tensor_tensor(cn[:, :, g * GH * HD:(g + 1) * GH * HD].rearrange("p t (h d) -> p t h d", d=HD),
                                whole[:, :, :, 0:HD], rden[:, :, :].unsqueeze(3).broadcast_to([P, NT, GH, HD]),
                                ALU.mult).then_inc(ctx_normed, 1)

            def ending(b, slot, i):
                n = [0]
                done = lambda x: DVE_C * b + x

                def step(ins, chained=True):
                    n[0] += 1
                    ins.then_inc(c_dve, 1)
                    if chained:
                        settle()

                def settle():
                    hold_apart(dve, c_dve, done(n[0]))

                def stats(x, at):
                    n[0] = at
                    settle()
                    for t in range(NT):
                        step(v.bn_stats(st[:, t, :], x[:, t, :]), False)

                def aggregate(at):
                    n[0] = at
                    settle()
                    for t in range(NT):
                        step(v.bn_aggr(mv[:, t, :], st[:, t, :]), False)

                def normalize(dst, x, at, ready):
                    n[0] = at
                    settle()
                    hold_apart(dve, c_pool, POOL_C * b + ready)
                    for t in range(NT):
                        step(v.tensor_scalar(dst[:, t, :], x[:, t, :], mv[:, t, 0:1], rstd[:, t:t + 1],
                                             ALU.subtract, ALU.mult), False)

                product = MB[:, :].rearrange("p (t n) -> p t n", t=NT)
                here = (slot, i)
                if here == (6, 3):
                    hold(dve, c_pe, PE_C * b + 2)
                    hold_apart(dve, c_pool, POOL_C * b + 1)
                    hold_apart(dve, out_done, 16 * b + 16)
                    step(v.tensor_tensor(x1[:, :, :], product, hs_bo[:, :, :], ALU.add), False)
                if here == (7, 2):
                    stats(x1, 1)
                if here == (7, 3):
                    aggregate(5)
                if here == (8, 2):
                    normalize(x1, x1, 9, 4)
                if here == (10, 2):
                    hold_apart(dve, c_pool, POOL_C * b + 6)
                    stats(x1, 13)
                if here == (10, 3):
                    aggregate(17)
                if here == (11, 1):
                    normalize(x2, x1, 21, 8)
                if here in QUANTIZE_AT:
                    if here == (12, 1):
                        hold_apart(dve, c_act, ACT_C * b + 3)
                    quantize(xq[:, :, :], xb[:, :, :], q1[:, :, :], q2[:, :, :], None, rs_sb[:, 0:1], step,
                             QUANTIZE_AT[here], n, 25 - 1, settle)
                if here == (15, 0):
                    hold(dve, c_act, ACT_C * b + 5)
                    n[0] = 33
                    step(v.tensor_tensor(xb[:, :, :], xb[:, :, :], bc(fb_sb), ALU.add))
                    step(v.tensor_tensor(x2[:, :, :], x2[:, :, :], xb[:, :, :], ALU.add), False)
                if here == (15, 1):
                    stats(x2, 35)
                if here == (15, 2):
                    aggregate(39)
                if here == (15, 4):
                    normalize(x1, x2, 43, 10)

            k_stacks(0, 0, 0)
            for j in range(GH):
                fix_diagonal(0, 0, j)
                for t in range(NT):
                    complete(0, 0, j, t)
                    if t % 2 == 1:
                        place_products(2 * j + t // 2)
                    if (j, t) == (0, 3):
                        value_factors()
                    if t == 1:
                        k_stacks(0, (j + 1) // GH, (j + 1) % GH)
            split_maxima(0, 0)

            def body(b, first=False, last=False):
                for c in range(NG):
                    more = not (last and c == NG - 1)
                    for j in range(GH):
                        n_ = 4 * (c + 1) + j + 1
                        if more:
                            fix_diagonal(b, c + 1, j)
                        for t in range(NT):
                            if more:
                                complete(b, c + 1, j, t)
                            if (j, t) == (0, 1 if more else 0):
                                copy_maxima(b, c)
                            if t == 1 and not (last and n_ >= H):
                                k_stacks(b, n_ // 4, n_ % 4)
                            if (j, t) == (3, 1) and not (first and c == 0):
                                norm_contexts(b, c - 1)
                            if not first:
                                ending(b - 1, 4 * c + j, t)
                            if first and c == 1:
                                quantize_kernel(4 * j + t)
                    if more:
                        split_maxima(b, c + 1)
                    if c == NG - 1 and not first:
                        ending(b - 1, 15, 4)

            body(0, first=True)
            with dve.Fori(1, B - 1) as b:
                body(b)
            body(B - 1, last=True)
            norm_contexts(B - 1, NG - 1)
            for slot in range(16):
                for i in range(5):
                    ending(B - 1, slot, i)


def _constants(np):
    pos = np.arange(S) - (S - 1) / 2
    far = np.exp(-DECAY * pos)
    fac_q, fac_k = np.ones((2, P, 2, S))
    fac_q[:HD * CH] = SCALE
    fac_q[HD * CH:, 0], fac_q[HD * CH:, 1] = ENT * SCALE * far, ENT * SCALE / far
    fac_k[HD * CH:, 0], fac_k[HD * CH:, 1] = 1 / far, far
    q, k = np.arange(P)[:, None], np.arange(P)[None, :]
    diagfix = np.where(q >= k, 1.0, np.exp(-2 * DECAY * (k - q)))
    kmask = np.zeros((P, 2))
    for row, n in GROUPS:
        for i in range(n * R):
            kmask[row + i, i % R // HD] = 1
    return {"fac_q": fac_q, "fac_k": fac_k, "ident": np.eye(P), "diagfix": diagfix, "kmask": kmask}


def kernel(**inputs):
    import numpy as np
    import concourse.bacc as _bacc
    from concourse.bass_utils import run_bass_kernel_spmd as _run

    a = {n.removeprefix("L0_"): np.asarray(x) for n, x in inputs.items()}
    w = {n.removeprefix("attn_"): x for n, x in a.items()}
    f32 = np.float32
    tokens = w["hidden_states"].reshape(B * S, D)

    def chunked(x, kind):
        return x.reshape(H // CH, CH, HD, *x.shape[1:]).swapaxes(1, 2)

    def rows(plain, entangled):
        x = np.concatenate([chunked(plain, 0), chunked(entangled, 1)], axis=1)
        return x.reshape(H // CH, P, *x.shape[3:])

    wq, wk = rows(w["Wq"], w["Weq"]), rows(w["Wk"], w["Wek"])
    bq, bk = rows(w["bq"], w["beq"]), rows(w["bk"], w["bek"])
    mixbd = np.zeros((H, HD, H, HD), f32)
    for h in range(H):
        mixbd[h, :, h, :] = w["mix_w"][h].T
    arrays = {
        "hs": tokens, "hsT": tokens.T,
        "wqk": np.stack([wq[0], wk[0], wq[1], wk[1]]).transpose(2, 0, 1),
        "bqk": np.stack([bq[0], bk[0], bq[1], bk[1]]).T,
        "wv": w["Wv"].T, "wv_nat": w["Wv"], "mixbd": mixbd.reshape(D, D), "bv_col": w["bv"].reshape(D, 1),
        "mixb": w["mix_b"].reshape(D), "wap": np.concatenate([w["amp_w"], w["ph_w"]]).T,
        "bap": np.concatenate([w["amp_b"], w["ph_b"]]), "bv_row": w["bv"], "wo": w["Wo"].T, "bo": w["bo"],
        "ln_g": w["ln_g"], "ln_b": w["ln_b"], "kern": w["ffn_kernel"], "s_in": w["ffn_input_scale"],
        "s_k": w["ffn_kernel_scale"], "fbias": w["ffn_bias"],
    }
    arrays.update({n: x.astype(f32) for n, x in _constants(np).items()})
    arrays = {f"in_{n}": np.ascontiguousarray(x) for n, x in arrays.items()}

    nc = _bacc.Bacc("TRN2", target_bir_lowering=False, num_devices=1)
    args = {n.removeprefix("in_"): nc.dram_tensor(n, x.shape, mybir.dt.from_np(x.dtype), kind="ExternalInput").ap()
            for n, x in arrays.items()}
    scratch = nc.dram_tensor("stacks", (B, 2, H // CH, 2, 3, R, CH, S), bf16, kind="Internal").ap()
    out = nc.dram_tensor("out", (B, S, D), fp32, kind="ExternalOutput").ap()
    attention_block(nc, scratch=scratch, out=out, **args)
    r = _run(nc, [arrays], core_ids=[0])
    return r.results[0]["out"]
```
